# Optimizing a Trainium2 kernel written in Bass

```python
import numpy as np
import jax
import jax.numpy as jnp

def _softmax(x, axis=-1):
    return jax.nn.softmax(x, axis=axis)

def _gelu(x):
    return jax.nn.gelu(x, approximate=True)

def _silu(x):
    return jax.nn.silu(x)

def _sigmoid(x):
    return jax.nn.sigmoid(x)

def _layernorm(x, axis=-1, eps=1e-05):
    m = jnp.mean(x, axis=axis, keepdims=True)
    v = jnp.var(x, axis=axis, keepdims=True)
    return (x - m) / jnp.sqrt(v + eps)

def _scatter_add(tgt, idx, src, axis=0):
    return tgt.at[idx].add(src)

def _segment_sum(src, seg, n):
    return jax.ops.segment_sum(src, seg, n)
kernel_name = 'mk_adj_resnorm_d2_adj_r2_a3da42'

def setup_inputs(seed: int=0):
    np.random.seed(seed)
    _w = jnp.asarray

    def _rec_inputs():
        import jax
        import jax.numpy as jnp
        _gk = jax.random.key(seed)
        x = -9.806e-05 + 1 * jax.random.normal(jax.random.fold_in(_gk, 1), (4096, 64), jnp.float32)
        _a = jax.random.bernoulli(jax.random.fold_in(_gk, 2), 0.00390625, (4096, 4096))
        _a = jnp.logical_or(_a, jnp.swapaxes(_a, -1, -2))
        _a = jnp.logical_or(_a, jnp.eye(4096, dtype=bool))
        _af = _a.astype(jnp.float32)
        _af = _af * jax.random.uniform(jax.random.fold_in(_gk, 3), (4096, 4096), jnp.float32, 0.05, 5.41998)
        adj = _af
        return (x, adj)
    x, adj = _rec_inputs()

    def _L0_gnn_setup():
        import jax, jax.numpy as jnp
        import numpy as np
        N = 4096
        H = 64
        ALPHA = 0.2
        NEG_INF = -9000000000000000.0

        def gru_cell(x, h, w_ih, w_hh, b_ih, b_hh):
            gi = x @ w_ih.T + b_ih
            gh = h @ w_hh.T + b_hh
            ir, iz, inn = jnp.split(gi, 3, axis=1)
            hr, hz, hn = jnp.split(gh, 3, axis=1)
            r = jax.nn.sigmoid(ir + hr)
            z = jax.nn.sigmoid(iz + hz)
            n = jnp.tanh(inn + r * hn)
            return (1.0 - z) * n + z * h

        def gat(h, node_adj, edge_adj, W, a):
            hw = h @ W
            h_plus = (node_adj > 0).astype(hw.dtype) @ hw
            h_minus = (node_adj < 0).astype(hw.dtype) @ hw
            e_plus = jax.nn.leaky_relu(jnp.concatenate([h_plus, h_minus], axis=1) @ a, ALPHA)
            e_minus = jax.nn.leaky_relu(jnp.concatenate([h_minus, h_plus], axis=1) @ a, ALPHA)
            att = jnp.where(edge_adj > 0, e_plus, NEG_INF)
            att = jnp.where(edge_adj < 0, e_minus, att)
            att = jax.nn.softmax(att, axis=1)
            return att * edge_adj @ hw
        key = jax.random.key(seed)
        ks = jax.random.split(key, 12)
        f32 = jnp.float32
        inp = {'h': jax.random.normal(ks[0], (N, H), f32), 'node_adj': jax.random.normal(ks[1], (N, N), f32), 'edge_adj': jax.random.normal(ks[2], (N, N), f32), 'W_gat': jax.random.normal(ks[3], (H, H), f32) * (1.414 * np.sqrt(6.0 / (2 * H))), 'a_gat': jax.random.normal(ks[4], (2 * H, 1), f32) * (1.414 * np.sqrt(6.0 / (2 * H + 1))), 'w_ih_e': jax.random.normal(ks[5], (3 * H, 2 * H), f32) * 0.01, 'w_hh_e': jax.random.normal(ks[6], (3 * H, H), f32) * 0.01, 'b_ih_e': jnp.zeros((3 * H,), f32), 'b_hh_e': jnp.zeros((3 * H,), f32), 'w_ih_n': jax.random.normal(ks[7], (3 * H, H), f32) * 0.01, 'w_hh_n': jax.random.normal(ks[8], (3 * H, H), f32) * 0.01, 'b_ih_n': jnp.zeros((3 * H,), f32), 'b_hh_n': jnp.zeros((3 * H,), f32)}
        return inp
    _L0_gnn_all = _L0_gnn_setup()
    _L0_gnn_in = {k: v for k, v in _L0_gnn_all.items() if k in ('W_gat', 'a_gat', 'w_ih_e', 'w_hh_e', 'b_ih_e', 'b_hh_e', 'w_ih_n', 'w_hh_n', 'b_ih_n', 'b_hh_n')}
    del _L0_gnn_all

    def _L1_gnn_setup():
        import jax, jax.numpy as jnp
        import numpy as np
        N = 5000
        DIM = 64
        F_CONST = 1.0
        B_CONST = 0.1
        R_CONST = 0.01
        key = jax.random.key(seed)
        k1, k2 = jax.random.split(key)
        t = jnp.zeros((1,), dtype=jnp.float32)
        x = jax.random.uniform(k1, (N, DIM), dtype=jnp.float32)
        A = jax.random.uniform(k2, (N, N), dtype=jnp.float32)
        return {'t': t, 'x': x, 'A': A}
    _L1_gnn_all = _L1_gnn_setup()
    _L1_gnn_in = {k: v for k, v in _L1_gnn_all.items() if k in ('t',)}
    del _L1_gnn_all
    return {'x': x, 'adj': adj, 'L0_gnn_W_gat': _L0_gnn_in['W_gat'], 'L0_gnn_a_gat': _L0_gnn_in['a_gat'], 'L0_gnn_w_ih_e': _L0_gnn_in['w_ih_e'], 'L0_gnn_w_hh_e': _L0_gnn_in['w_hh_e'], 'L0_gnn_b_ih_e': _L0_gnn_in['b_ih_e'], 'L0_gnn_b_hh_e': _L0_gnn_in['b_hh_e'], 'L0_gnn_w_ih_n': _L0_gnn_in['w_ih_n'], 'L0_gnn_w_hh_n': _L0_gnn_in['w_hh_n'], 'L0_gnn_b_ih_n': _L0_gnn_in['b_ih_n'], 'L0_gnn_b_hh_n': _L0_gnn_in['b_hh_n'], 'L1_gnn_t': _L1_gnn_in['t']}

def reference(x, adj, L0_gnn_W_gat, L0_gnn_a_gat, L0_gnn_w_ih_e, L0_gnn_w_hh_e, L0_gnn_b_ih_e, L0_gnn_b_hh_e, L0_gnn_w_ih_n, L0_gnn_w_hh_n, L0_gnn_b_ih_n, L0_gnn_b_hh_n, L1_gnn_t):
    import jax
    import jax.numpy as jnp

    def _L0_gnn_ref(h, node_adj, edge_adj, W_gat, a_gat, w_ih_e, w_hh_e, b_ih_e, b_hh_e, w_ih_n, w_hh_n, b_ih_n, b_hh_n):
        import jax, jax.numpy as jnp
        import numpy as np
        N = 4096
        H = 64
        ALPHA = 0.2
        NEG_INF = -9000000000000000.0

        def gru_cell(x, h, w_ih, w_hh, b_ih, b_hh):
            gi = x @ w_ih.T + b_ih
            gh = h @ w_hh.T + b_hh
            ir, iz, inn = jnp.split(gi, 3, axis=1)
            hr, hz, hn = jnp.split(gh, 3, axis=1)
            r = jax.nn.sigmoid(ir + hr)
            z = jax.nn.sigmoid(iz + hz)
            n = jnp.tanh(inn + r * hn)
            return (1.0 - z) * n + z * h

        def gat(h, node_adj, edge_adj, W, a):
            hw = h @ W
            h_plus = (node_adj > 0).astype(hw.dtype) @ hw
            h_minus = (node_adj < 0).astype(hw.dtype) @ hw
            e_plus = jax.nn.leaky_relu(jnp.concatenate([h_plus, h_minus], axis=1) @ a, ALPHA)
            e_minus = jax.nn.leaky_relu(jnp.concatenate([h_minus, h_plus], axis=1) @ a, ALPHA)
            att = jnp.where(edge_adj > 0, e_plus, NEG_INF)
            att = jnp.where(edge_adj < 0, e_minus, att)
            att = jax.nn.softmax(att, axis=1)
            return att * edge_adj @ hw
        d_node = jnp.diag(node_adj)
        d_edge = jnp.diag(edge_adj)
        A_node = node_adj - jnp.diag(d_node)
        A_edge = edge_adj - jnp.diag(d_edge)
        node_support = jnp.concatenate([(A_node > 0).astype(h.dtype) @ h, (A_node < 0).astype(h.dtype) @ h], axis=1)
        edge_output = gru_cell(node_support, h, w_ih_e, w_hh_e, b_ih_e, b_hh_e)
        edge_support = gat(h, A_node, A_edge, W_gat, a_gat)
        node_output = gru_cell(edge_support, h, w_ih_n, w_hh_n, b_ih_n, b_hh_n)
        return d_edge[:, None] * edge_output + d_node[:, None] * node_output

    def _L1_gnn_ref(t, x, A):
        import jax, jax.numpy as jnp
        import numpy as np
        N = 5000
        DIM = 64
        F_CONST = 1.0
        B_CONST = 0.1
        R_CONST = 0.01
        Ax = A @ x
        outer = R_CONST * jnp.sum(x * Ax, axis=1, keepdims=True)
        return F_CONST - B_CONST * x - outer
    x = _layernorm(x + _L0_gnn_ref(x, adj, adj, L0_gnn_W_gat, L0_gnn_a_gat, L0_gnn_w_ih_e, L0_gnn_w_hh_e, L0_gnn_b_ih_e, L0_gnn_b_hh_e, L0_gnn_w_ih_n, L0_gnn_w_hh_n, L0_gnn_b_ih_n, L0_gnn_b_hh_n), axis=-1)
    x = _layernorm(x + _L1_gnn_ref(L1_gnn_t, x, adj), axis=-1)
    return x

_drawn_inputs = setup_inputs


def setup_inputs(seed=0):
    import zlib

    import numpy as np

    out = dict(_drawn_inputs(seed))
    spreads = {'L0_gnn_b_ih_e': (0.0, 0.1),
     'L0_gnn_b_hh_e': (0.0, 0.339),
     'L0_gnn_b_ih_n': (0.0, 0.1),
     'L0_gnn_b_hh_n': (0.0, 0.326)}
    factors = {'L0_gnn_w_hh_e': 3.096, 'L0_gnn_w_hh_n': 3.092}
    for name, (base, spread) in spreads.items():
        noise = np.random.default_rng([zlib.crc32(name.encode()), seed]).standard_normal(out[name].shape)
        drawn = base * np.exp(spread * noise) if base else spread * noise
        out[name] = jnp.asarray(drawn.astype(out[name].dtype))
    for name, factor in factors.items():
        out[name] = (out[name] * factor).astype(out[name].dtype)
    return out
```

```python
import concourse.bass as bass
from concourse import mybir
from contextlib import ExitStack

NEG_INF = -9.0e15
ALPHA = 0.2
EPS = 1e-5
AWAY = 1.0 + 2.0 ** -12


def gnn_ode_kernel(nc: bass.Bass, adj_t, x_rows_d, x_t_d, diag_d, gat_d, w_gat_t_d, w_plus_d,
                   w_minus_d, w_h_d, bias_d, out):
    fp32, f32r, i32 = mybir.dt.float32, mybir.dt.float32r, mybir.dt.int32
    ALU, ACT, AX = mybir.AluOpType, mybir.ActivationFunctionType, mybir.AxisListType

    BLOCKS, UNITS, P, UT, BI = adj_t.shape
    N = BLOCKS * BI
    TILES = N // P
    CH = BI // P
    UPB = UNITS // BLOCKS
    H = 64
    UW = UT * BI
    RAW = 8
    RING = 4

    ctx = ExitStack()
    with ctx:
        def sb(name, shape, dt=fp32):
            return ctx.enter_context(nc.sbuf_tensor(name, shape, dt))

        def sem(name):
            return ctx.enter_context(nc.semaphore(name))

        raw = sb("raw", [P, RAW, UW])
        mask = sb("mask", [P, RING, UW], f32r)
        hi = sb("hi", [P, RING, UW], f32r)
        lo = sb("lo", [P, RING, UW], f32r)
        h_split = sb("h_split", [P, TILES, 2 * H], f32r)
        x1_split = sb("x1_split", [P, TILES, 2 * H], f32r)
        x_rows = sb("x_rows", [P, TILES, H])
        x1_rows = sb("x1_rows", [P, TILES, H])
        ax_part = sb("ax_part", [P, BLOCKS, BI])
        diag = sb("diag", [P, TILES])
        xt_raw = sb("xt_raw", [P, BI])
        xt_hi = sb("xt_hi", [P, BI])
        xt_split = sb("xt_split", [P, BI], f32r)
        ones = sb("ones", [P, P], f32r)
        ident = sb("ident", [P, P])
        pair_ident = sb("pair_ident", [P, H])
        zero_w = sb("zero_w", [P, P], f32r)
        gat = sb("gat", [H, 3 * H + 2])
        w_gat_t = sb("w_gat_t", [H, 2 * H])
        w_plus = sb("w_plus", [P, 3 * H])
        w_minus = sb("w_minus", [P, 3 * H])
        w_value = sb("w_value", [P, 3 * H])
        a_plus = sb("a_plus", [P, 2])
        a_minus = sb("a_minus", [P, 2])
        w_h_raw = sb("w_h_raw", [P, 4 * P])
        w_h_hi = sb("w_h_hi", [P, 4 * P], f32r)
        w_h_lo = sb("w_h_lo", [P, 4 * P], f32r)
        bias_raw = sb("bias_raw", [H, 4 * P])
        bias_split = sb("bias_split", [H, 4 * P], f32r)
        plus_sb = sb("plus_sb", [P, BI])
        value_sb = sb("value_sb", [P, BI])
        count_sb = sb("count_sb", [1, BI])
        minus_sb = sb("minus_sb", [P, BI])
        nvalue_sb = sb("nvalue_sb", [P, BI])
        ncount_sb = sb("ncount_sb", [1, BI])
        gates = sb("gates", [P, CH, 4, P])
        vals = sb("vals", [P, CH, 388])
        above = sb("above", [P, UNITS])
        above_max = sb("above_max", [P, 1])
        above_all = sb("above_all", [1, 1])
        has_minus = sb("has_minus", [1, BLOCKS], i32)
        leaky = sb("leaky", [P, CH, 2])
        absent = sb("absent", [P, CH, 2])
        top = sb("top", [P, CH, 1])
        expo = sb("expo", [P, CH, 3])
        cnt = sb("cnt", [P, CH, 3])
        norm = sb("norm", [P, CH, 1])
        att = sb("att", [P, CH, 3])
        y = sb("y", [P, CH, H])
        sq = sb("sq", [P, CH, H])
        mean = sb("mean", [P, CH, 1])
        var = sb("var", [P, CH, 1])
        rstd = sb("rstd", [P, CH, 1])
        neg_half = sb("neg_half", [P, CH, 1])
        ax_sb = sb("ax_sb", [P, BI])
        res = sb("res", [P, 2, CH, H])
        c_raw = gates[:, 0:1].rearrange("p a b c -> p (a b c)")
        c_mask = sb("c_mask", [P, BI], f32r)
        c_hi = sb("c_hi", [P, BI], f32r)
        c_lo = sb("c_lo", [P, BI], f32r)

        bank = [ctx.enter_context(nc.psum_tensor(f"bank{n}", [P, BI], fp32)) for n in range(8)]
        PLUS, COUNT, VALUE, AX1 = bank[0:4]
        EA, EB = bank[4:6], bank[6:8]

        s_raw = [sem(f"s_raw{n}") for n in range(RAW)]
        s_setup_d = sem("s_setup_d")
        s_const = sem("s_const")
        s_w = sem("s_w")
        s_wsplit = sem("s_wsplit")
        s_diag = sem("s_diag")
        s_tile = sem("s_tile")
        s_mask = sem("s_mask")
        s_hi = sem("s_hi")
        s_lo = sem("s_lo")
        s_free = sem("s_free")
        s_evac = sem("s_evac")
        s_above = sem("s_above")
        s_above_t = sem("s_above_t")
        s_flag = sem("s_flag")
        s_seen = sem("s_seen")
        s_xt_d = sem("s_xt_d")
        s_xt = sem("s_xt")
        s_ep = sem("s_ep")
        s_ep_out = sem("s_ep_out")
        s_expo = sem("s_expo")
        s_exp = sem("s_exp")
        s_gin = sem("s_gin")
        s_act = sem("s_act")
        s_nin = sem("s_nin")
        s_var = sem("s_var")
        s_rstd = sem("s_rstd")
        s_x1 = sem("s_x1")
        s_dve = sem("s_dve")
        s_pool = sem("s_pool")
        c_dma = sem("c_dma")
        c_diag = sem("c_diag")
        c_tile = sem("c_tile")
        c_dve = sem("c_dve")
        c_chain = sem("c_chain")
        c_used = sem("c_used")
        c_out = sem("c_out")
        s_hi2 = sem("s_hi2")
        s_lo2 = sem("s_lo2")
        s_free2 = sem("s_free2")
        s_ax = sem("s_ax")
        s_ax_sb = sem("s_ax_sb")
        s_fin = sem("s_fin")
        s_fin_rd = sem("s_fin_rd")
        s_res = sem("s_res")
        s_out = [sem(f"s_out{n}") for n in range(2)]

        PAIRS = [(J, I) for J in reversed(range(BLOCKS)) for I in range(J + 1)]
        UNITS2 = [(J, I, h) for J, I in PAIRS for h in range(UPB)]
        LOADS1 = BLOCKS * UNITS

        block = ctx.enter_context(nc.Block())

        def seen(eng):
            eng.sem_inc(s_seen, 1)

        def bc(ap, n):
            return ap.to_broadcast([P, CH, n])

        @block.sync
        def _(eng):
            def load(slot, src):
                eng.dma_start(raw[:, slot, :], src.rearrange("p t i -> p (t i)")).then_inc(s_raw[slot], 16)

            eng.dma_start(x_rows[:, :, :], x_rows_d).then_inc(s_setup_d, 16)
            for u in range(RAW):
                load(u, adj_t[0, u, :, :, :])
            with eng.Fori(0, BLOCKS - 1) as I:
                for u in range(UNITS):
                    eng.wait_ge(s_lo, UNITS * I + u + 1)
                    n = u + RAW
                    if n < UNITS:
                        load(n % RAW, adj_t[I, n, :, :, :])
                    else:
                        load(n % RAW, adj_t[I + 1, n - UNITS, :, :, :])
            for u in range(UNITS - RAW):
                eng.wait_ge(s_lo, UNITS * (BLOCKS - 1) + u + 1)
                load(u % RAW, adj_t[BLOCKS - 1, u + RAW, :, :, :])
            for n, (J, I, h) in enumerate(UNITS2):
                if n < RAW:
                    eng.wait_ge(s_lo, LOADS1 - RAW + n + 1)
                else:
                    eng.wait_ge(s_lo2, n - RAW + 1)
                load(n % RAW, adj_t[I, UPB * J + h, :, :, :])

        @block.gpsimd
        def _(eng):
            eng.memset(ident[:, :], 0.0).then_inc(s_pool, 1)
            eng.memset(pair_ident[:, :], 0.0).then_inc(s_pool, 1)
            eng.memset(neg_half[:, :, :], -0.5).then_inc(s_const, 1)
            eng.wait_ge(s_pool, 2)
            eng.affine_select(out=ident[:, :], in_=ident[:, :], compare_op=ALU.not_equal, fill=1.0,
                              base=0, pattern=[[-1, P]], channel_multiplier=1).then_inc(s_const, 1)
            eng.affine_select(out=pair_ident[:, :], in_=pair_ident[:, :], compare_op=ALU.not_equal,
                              fill=1.0, base=0, pattern=[[-1, H]], channel_multiplier=1).then_inc(s_pool, 1)
            eng.wait_ge(s_pool, 3)
            eng.affine_select(out=pair_ident[:, :], in_=pair_ident[:, :], compare_op=ALU.not_equal,
                              fill=1.0, base=-H, pattern=[[-1, H]], channel_multiplier=1).then_inc(s_const, 1)
            POOL0, POOL_PER = 3, 2

            def zero_diagonal(ap, q, s):
                part = ap[:, q * P:(q + 1) * P]
                eng.affine_select(out=part, in_=part, compare_op=ALU.not_equal, fill=0.0, base=0,
                                  pattern=[[-1, P]], channel_multiplier=1).then_inc(s, 1)

            with eng.Fori(0, BLOCKS) as I:
                for u in range(UNITS):
                    eng.wait_ge(s_raw[u % RAW], 16 * ((UNITS // RAW) * I + u // RAW + 1))
                    seen(eng)
                    with eng.If(I == u // UPB):
                        for t in range(UT):
                            zero_diagonal(raw[:, u % RAW, t * BI:(t + 1) * BI], UT * (u % UPB) + t, s_diag)
                        eng.wait_ge(s_diag, CH * I + UT * (u % UPB + 1))
                    eng.sem_inc(s_tile, 1)
                eng.dma_start(xt_raw[:, :], x_t_d[I]).then_inc(s_xt_d, 16)
                eng.wait_ge(s_xt_d, 16 * (I + 1))
                eng.wait_ge(s_ep, CH * I + 1)
                seen(eng)
                eng.tensor_copy(xt_split[:, :], xt_raw[:, :]).then_inc(s_pool, 1)
                eng.wait_ge(s_pool, POOL_PER * I + POOL0 + 1)
                seen(eng)
                eng.tensor_copy(xt_hi[H:P, :], xt_split[H:P, :].bitcast(fp32)).then_inc(s_pool, 1)
                eng.wait_ge(s_pool, POOL_PER * I + POOL0 + 2)
                eng.tensor_tensor(xt_split[H:P, :], xt_raw[H:P, :], xt_hi[H:P, :],
                                  ALU.subtract).then_inc(s_xt, 1)
                eng.wait_ge(s_xt, I + 1)
                eng.wait_ge(s_flag, I + 1)
                seen(eng)
                flag = eng.value_load(has_minus[0:1, bass.ds(I, 1)])
                with eng.If(flag > 0):
                    for J in range(BLOCKS):
                        for q in range(CH):
                            k = CH * J + q
                            eng.wait_ge(c_dma, 16 * (TILES * I + k + 1))
                            seen(eng)
                            with eng.If(I == J):
                                zero_diagonal(c_raw, q, c_diag)
                                eng.wait_ge(c_diag, CH * I + q + 1)
                            eng.sem_inc(c_tile, 1)
                with eng.Else():
                    eng.sem_inc(c_tile, TILES)
                    eng.sem_inc(c_diag, CH)
                eng.wait_ge(s_var, I + 1)
                eng.tensor_tensor(rstd[:, :, :], var[:, :, :], neg_half[:, :, :], ALU.pow).then_inc(s_rstd, 1)
            for n in range(BLOCKS):
                J = BLOCKS - 1 - n
                eng.wait_ge(s_var, BLOCKS + n + 1)
                eng.tensor_tensor(rstd[:, :, :], var[:, :, :], neg_half[:, :, :], ALU.pow).then_inc(s_rstd, 1)
                eng.wait_ge(s_res, n + 1)
                eng.dma_start(out[J * BI:(J + 1) * BI, :].rearrange("(c p) f -> p c f", p=P),
                              res[:, n % 2, :, :]).then_inc(s_out[n % 2], 16)
            for done in s_out:
                eng.wait_ge(done, 16 * BLOCKS // 2)

        @block.scalar
        def _(eng):
            eng.dma_start(gat[:, :], gat_d).then_inc(s_setup_d, 16)
            eng.dma_start(w_gat_t[:, :], w_gat_t_d).then_inc(s_setup_d, 16)
            eng.dma_start(w_plus[:, :], w_plus_d).then_inc(s_setup_d, 16)
            eng.dma_start(w_minus[:, :], w_minus_d).then_inc(s_setup_d, 16)
            eng.dma_start(w_h_raw[:, :], w_h_d).then_inc(s_setup_d, 16)
            eng.dma_start(bias_raw[:, :], bias_d).then_inc(s_setup_d, 16)
            eng.dma_start(diag[:, :], diag_d).then_inc(s_setup_d, 16)
            eng.wait_ge(s_setup_d, 8 * 16)
            eng.activation(h_split[:, :, 0:H], x_rows[:, :, :], ACT.Copy).then_inc(s_wsplit, 1)
            eng.activation(w_h_hi[:, :], w_h_raw[:, :], ACT.Copy).then_inc(s_wsplit, 1)

            with eng.Fori(0, BLOCKS) as I:
                for u in range(UNITS):
                    g = UNITS * I + u
                    eng.wait_ge(s_tile, g + 1)
                    eng.wait_ge(s_free, g + 1)
                    eng.activation(hi[:, u % RING, :], raw[:, u % RAW, :], ACT.Copy,
                                   scale=AWAY).then_inc(s_hi, 1)
                eng.wait_ge(s_free, UNITS * (I + 1) + RING)
                eng.activation(plus_sb[:, :], PLUS[:, :], ACT.Copy).then_inc(s_evac, 1)
                eng.activation(ax_part[:, bass.ds(I, 1), :].rearrange("p a i -> p (a i)"), AX1[:, :],
                               ACT.Copy).then_inc(s_evac, 1)
                eng.wait_ge(s_flag, I + 1)
                seen(eng)
                flag = eng.value_load(has_minus[0:1, bass.ds(I, 1)])
                with eng.If(flag > 0):
                    with eng.Fori(0, UNITS) as u:
                        for t in range(UT):
                            eng.wait_ge(c_used, TILES * I + UT * u + t + 1)
                            eng.dma_start(c_raw, adj_t[I, u, :, t, :]).then_inc(c_dma, 16)
                with eng.Else():
                    eng.sem_inc(c_dma, 16 * TILES)
                for c in range(CH):
                    eng.wait_ge(s_ep, CH * I + c + 2)
                    eng.activation(gates[:, c, :, :].rearrange("p g n -> p (g n)"), EA[c % 2][:, :],
                                   ACT.Copy).then_inc(s_ep_out, 1)
                    with eng.If(flag > 0):
                        eng.activation(vals[:, c, :], EB[c % 2][:, 0:388], ACT.Copy).then_inc(s_ep_out, 1)
                    with eng.Else():
                        eng.activation(vals[:, c, 0:195], EB[c % 2][:, 0:195], ACT.Copy).then_inc(s_ep_out, 1)
                eng.wait_ge(s_expo, I + 1)
                eng.activation(expo[:, :, :], expo[:, :, :], ACT.Exp).then_inc(s_exp, 1)
                eng.wait_ge(s_gin, I + 1)
                eng.activation(gates[:, :, 0:2, :], gates[:, :, 0:2, :], ACT.Tanh,
                               scale=0.5).then_inc(s_act, 1)
                eng.wait_ge(s_nin, I + 1)
                eng.activation(gates[:, :, 2, :], gates[:, :, 2, :], ACT.Tanh).then_inc(s_act, 1)
            fin = 0
            for n, (J, I, h) in enumerate(UNITS2):
                eng.wait_ge(s_raw[n % RAW], 16 * (LOADS1 // RAW + n // RAW + 1))
                eng.wait_ge(s_free2, n + 1)
                eng.activation(hi[:, n % RING, :], raw[:, n % RAW, :], ACT.Copy).then_inc(s_hi2, 1)
                if I == J and h == UPB - 1:
                    eng.wait_ge(s_ax, fin + 1)
                    if fin:
                        eng.wait_ge(s_fin, fin)
                    eng.activation(ax_sb[:, :], bank[J][:, :], ACT.Copy).then_inc(s_ax_sb, 1)
                    fin += 1

        @block.vector
        def _(eng):
            eng.wait_ge(s_setup_d, 8 * 16)
            eng.memset(mask[:, 0, 0:P].bitcast(fp32), 1.0).then_inc(s_dve, 1)
            eng.memset(zero_w[:, :].bitcast(fp32), 0.0).then_inc(s_const, 1)
            eng.memset(bias_split[:, :].bitcast(fp32), 0.0).then_inc(s_dve, 1)
            eng.wait_ge(s_dve, 2)
            eng.tensor_copy(ones[:, :], mask[:, 0, 0:P].bitcast(fp32)).then_inc(s_const, 1)
            eng.wait_ge(s_wsplit, 2)
            eng.tensor_tensor(h_split[:, :, H:2 * H], x_rows[:, :, :], h_split[:, :, 0:H].bitcast(fp32),
                              ALU.subtract).then_inc(s_wsplit, 1)
            eng.tensor_tensor(w_h_lo[:, :], w_h_raw[:, :], w_h_hi[:, :].bitcast(fp32),
                              ALU.subtract).then_inc(s_wsplit, 1)
            eng.tensor_copy(bias_split[0:2, :], bias_raw[0:2, :]).then_inc(s_wsplit, 1)
            eng.tensor_copy(bias_split[32:34, :], bias_raw[32:34, :]).then_inc(s_dve, 1)
            eng.wait_ge(s_dve, 3)
            eng.tensor_tensor(bias_split[32:34, :], bias_raw[32:34, :], bias_split[32:34, :].bitcast(fp32),
                              ALU.subtract).then_inc(s_wsplit, 1)
            eng.wait_ge(s_w, 1)
            eng.tensor_copy(w_value[:, :], EA[0][:, 0:3 * H]).then_inc(s_wsplit, 1)
            eng.tensor_copy(a_plus[:, :], EA[0][:, 3 * H:3 * H + 2]).then_inc(s_wsplit, 1)
            eng.tensor_copy(a_minus[:, 0:1], EA[0][:, 3 * H + 1:3 * H + 2]).then_inc(s_wsplit, 1)
            eng.tensor_copy(a_minus[:, 1:2], EA[0][:, 3 * H:3 * H + 1]).then_inc(s_wsplit, 1)

            BASE = 3
            PER_BLOCK = 34
            links = [0]

            def link(ins, at):
                links[0] += 1
                ins.then_inc(s_dve, 1)
                eng.wait_ge(s_dve, at + links[0])

            def layer_norm(at, norm_before):
                link(eng.reduce_sum(mean[:, :, :], y[:, :, :], AX.X), at)
                link(eng.tensor_scalar(mean[:, :, :], mean[:, :, :], 1.0 / H, None, ALU.mult), at)
                link(eng.tensor_tensor(y[:, :, :], y[:, :, :], bc(mean[:, :, :], H), ALU.subtract), at)
                link(eng.tensor_tensor(sq[:, :, :], y[:, :, :], y[:, :, :], ALU.mult), at)
                link(eng.reduce_sum(var[:, :, :], sq[:, :, :], AX.X), at)
                eng.tensor_scalar(var[:, :, :], var[:, :, :], 1.0 / H, EPS, ALU.mult, ALU.add).then_inc(s_var, 1)
                eng.wait_ge(s_rstd, norm_before + 1)

            with eng.Fori(0, BLOCKS) as I:
                for u in range(UNITS):
                    g = UNITS * I + u
                    eng.wait_ge(s_tile, g + 1)
                    eng.wait_ge(s_free, g + 1)
                    eng.wait_ge(s_hi, g + 1)
                    eng.tensor_scalar(mask[:, u % RING, :], raw[:, u % RAW, :], 0.0, None,
                                      ALU.is_gt).then_inc(s_mask, 1)
                    eng.tensor_tensor_reduce(out=lo[:, u % RING, :], in0=raw[:, u % RAW, :],
                                             in1=hi[:, u % RING, :].bitcast(fp32), scale=1.0, scalar=-3.0e38,
                                             op0=ALU.subtract, op1=ALU.max,
                                             accum_out=above[:, u:u + 1]).then_inc(s_lo, 1)
                at = PER_BLOCK * I + BASE
                links[0] = 0
                eng.wait_ge(s_free, UNITS * (I + 1) + RING)
                eng.tensor_copy(value_sb[:, :], VALUE[:, :]).then_inc(s_evac, 1)
                eng.tensor_copy(count_sb[:, :], COUNT[0:1, :]).then_inc(s_evac, 1)
                eng.wait_ge(s_lo, UNITS * (I + 1))
                eng.reduce_max(above_max[:, :], above[:, :], AX.X).then_inc(s_above, 1)
                eng.wait_ge(s_above_t, I + 1)
                link(eng.reduce_max(above_all[:, :], EB[0][0:1, 0:P], AX.X), at)
                eng.tensor_scalar(has_minus[0:1, bass.ds(I, 1)], above_all[:, :], 0.0, None,
                                  ALU.is_gt).then_inc(s_flag, 1)
                eng.wait_ge(s_flag, I + 1)
                seen(eng)
                flag = eng.value_load(has_minus[0:1, bass.ds(I, 1)])
                with eng.If(flag > 0):
                    with eng.Fori(0, TILES) as k:
                        n = TILES * I + k
                        eng.wait_ge(c_tile, n + 1)
                        eng.wait_ge(c_used, n + 1)
                        eng.tensor_scalar(c_mask[:, :], c_raw, 0.0, None, ALU.is_lt).then_inc(c_dve, 1)
                        eng.tensor_scalar(c_hi[:, :], c_raw, 0.0, None, ALU.min).then_inc(c_dve, 1)
                        eng.wait_ge(c_dve, 3 * n + 2)
                        eng.scalar_tensor_tensor(c_lo[:, :], c_raw, 0.0, c_hi[:, :].bitcast(fp32),
                                                 ALU.min, ALU.subtract).then_inc(c_dve, 1)
                    eng.wait_ge(c_used, TILES * (I + 1) + 1)
                    eng.tensor_copy(minus_sb[:, :], EA[0][:, :]).then_inc(c_out, 1)
                    eng.tensor_copy(ncount_sb[:, :], EA[1][0:1, :]).then_inc(c_out, 1)
                    eng.tensor_copy(nvalue_sb[:, :], EB[1][:, :]).then_inc(c_out, 1)
                with eng.Else():
                    eng.sem_inc(c_dve, 3 * TILES)
                    eng.sem_inc(c_out, 3)
                eng.wait_ge(s_ep_out, 2 * CH * (I + 1) + 1)
                link(eng.tensor_copy(cnt[:, :, 0:1], vals[:, :, 194:195]), at)
                seen(eng)
                with eng.If(flag > 0):
                    eng.tensor_copy(cnt[:, :, 1:2], vals[:, :, 195:196]).then_inc(s_dve, 1)
                with eng.Else():
                    eng.memset(cnt[:, :, 1:2], 0.0).then_inc(s_dve, 1)
                links[0] += 1
                eng.wait_ge(s_dve, at + links[0])
                link(eng.tensor_tensor(cnt[:, :, 2:3], cnt[:, :, 0:1], cnt[:, :, 1:2], ALU.add), at)
                link(eng.tensor_scalar(cnt[:, :, 2:3], cnt[:, :, 2:3], -1.0, float(N), ALU.mult, ALU.add), at)
                link(eng.scalar_tensor_tensor(leaky[:, :, :], vals[:, :, 192:194], ALPHA, vals[:, :, 192:194],
                                              ALU.mult, ALU.max), at)
                link(eng.tensor_scalar(absent[:, :, :], cnt[:, :, 0:2], 0.0, 4 * NEG_INF, ALU.is_le, ALU.mult), at)
                link(eng.tensor_tensor(leaky[:, :, :], leaky[:, :, :], absent[:, :, :], ALU.add), at)
                link(eng.tensor_tensor(top[:, :, :], leaky[:, :, 0:1], leaky[:, :, 1:2], ALU.max), at)
                link(eng.tensor_scalar(top[:, :, :], top[:, :, :], NEG_INF, None, ALU.max), at)
                link(eng.tensor_tensor(expo[:, :, 0:2], leaky[:, :, :], bc(top[:, :, :], 2), ALU.subtract), at)
                eng.tensor_scalar(expo[:, :, 2:3], top[:, :, :], -1.0, NEG_INF, ALU.mult, ALU.add).then_inc(s_expo, 1)
                eng.wait_ge(s_exp, I + 1)
                link(eng.tensor_tensor(cnt[:, :, :], cnt[:, :, :], expo[:, :, :], ALU.mult), at)
                link(eng.reduce_sum(norm[:, :, :], cnt[:, :, :], AX.X), at)
                link(eng.reciprocal(norm[:, :, :], norm[:, :, :]), at)
                link(eng.tensor_tensor(att[:, :, 0:2], expo[:, :, 0:2], bc(norm[:, :, :], 2), ALU.mult), at)
                link(eng.tensor_tensor(att[:, :, 2:3], att[:, :, 1:2], att[:, :, 0:1], ALU.subtract), at)
                for c in range(CH):
                    g3 = gates[:, c, 0:3, H:P]
                    v3 = vals[:, c, 0:3 * H].rearrange("p (g f) -> p g f", g=3)
                    eng.scalar_tensor_tensor(g3, v3, att[:, c, 0:1], g3, ALU.mult, ALU.add).then_inc(s_dve, 1)
                links[0] += CH
                eng.wait_ge(s_dve, at + links[0])
                seen(eng)
                with eng.If(flag > 0):
                    for c in range(CH):
                        g3 = gates[:, c, 0:3, H:P]
                        v3 = vals[:, c, 196:196 + 3 * H].rearrange("p (g f) -> p g f", g=3)
                        eng.scalar_tensor_tensor(g3, v3, att[:, c, 2:3], g3, ALU.mult, ALU.add).then_inc(c_chain, 1)
                with eng.Else():
                    eng.sem_inc(c_chain, CH)
                eng.wait_ge(c_chain, CH * (I + 1))
                eng.sem_inc(s_gin, 1)
                eng.wait_ge(s_act, 2 * I + 1)
                link(eng.scalar_tensor_tensor(gates[:, :, 3, :], gates[:, :, 0, :], 1.0, gates[:, :, 3, :],
                                              ALU.add, ALU.mult), at)
                eng.scalar_tensor_tensor(gates[:, :, 2, :], gates[:, :, 3, :], 0.5, gates[:, :, 2, :],
                                         ALU.mult, ALU.add).then_inc(s_nin, 1)
                eng.wait_ge(s_act, 2 * I + 2)
                xb = x_rows[:, bass.ds(CH * I, CH), :]
                for net in range(2):
                    eng.tensor_tensor(gates[:, :, 3, net * H:(net + 1) * H], xb,
                                      gates[:, :, 2, net * H:(net + 1) * H], ALU.subtract).then_inc(s_dve, 1)
                links[0] += 2
                eng.wait_ge(s_dve, at + links[0])
                link(eng.scalar_tensor_tensor(gates[:, :, 1, :], gates[:, :, 1, :], 1.0, gates[:, :, 3, :],
                                              ALU.add, ALU.mult), at)
                link(eng.scalar_tensor_tensor(gates[:, :, 2, :], gates[:, :, 1, :], 0.5, gates[:, :, 2, :],
                                              ALU.mult, ALU.add), at)
                link(eng.tensor_tensor(y[:, :, :], gates[:, :, 2, 0:H], gates[:, :, 2, H:P], ALU.add), at)
                link(eng.tensor_tensor(y[:, :, :], y[:, :, :],
                                       diag[:, bass.ds(CH * I, CH)].rearrange("p (c o) -> p c o", o=1).to_broadcast([P, CH, H]),
                                       ALU.mult), at)
                link(eng.tensor_tensor(y[:, :, :], y[:, :, :], xb, ALU.add), at)
                layer_norm(at, I)
                x1b = x1_rows[:, bass.ds(CH * I, CH), :]
                link(eng.tensor_tensor(x1b, y[:, :, :], bc(rstd[:, :, :], H), ALU.mult), at)
                x1h = x1_split[:, bass.ds(CH * I, CH), 0:H]
                eng.tensor_copy(x1h, x1b).then_inc(s_x1, 1)
                eng.wait_ge(s_x1, 2 * I + 1)
                eng.tensor_tensor(x1_split[:, bass.ds(CH * I, CH), H:2 * H], x1b, x1h.bitcast(fp32),
                                  ALU.subtract).then_inc(s_x1, 1)
            assert links[0] == PER_BLOCK, links[0]

            links[0] = 0
            at = BASE + PER_BLOCK * BLOCKS

            def finish(n):
                J = BLOCKS - 1 - n
                x1b = x1_rows[:, CH * J:CH * (J + 1), :]
                eng.wait_ge(s_fin, n + 1)
                axp = bank[BLOCKS - 1][:, 0:CH * H].rearrange("p (c f) -> p c f", c=CH)
                eng.tensor_tensor(sq[:, :, :], axp, x1b, ALU.mult).then_inc(s_fin_rd, 1)
                eng.wait_ge(s_fin_rd, n + 1)
                link(eng.reduce_sum(mean[:, :, :], sq[:, :, :], AX.X), at)
                link(eng.tensor_scalar(mean[:, :, :], mean[:, :, :], 0.01, None, ALU.mult), at)
                link(eng.tensor_scalar(y[:, :, :], x1b, -0.1, 1.0, ALU.mult, ALU.add), at)
                link(eng.tensor_tensor(y[:, :, :], y[:, :, :], bc(mean[:, :, :], H), ALU.subtract), at)
                link(eng.tensor_tensor(y[:, :, :], y[:, :, :], x1b, ALU.add), at)
                layer_norm(at, BLOCKS + n)
                if n >= 2:
                    eng.wait_ge(s_out[n % 2], 16 * (n // 2))
                eng.tensor_tensor(res[:, n % 2, :, :], y[:, :, :], bc(rstd[:, :, :], H),
                                  ALU.mult).then_inc(s_res, 1)

            fin = 0
            for n, (J, I, h) in enumerate(UNITS2):
                eng.wait_ge(s_hi2, n + 1)
                eng.tensor_tensor(lo[:, n % RING, :], raw[:, n % RAW, :], hi[:, n % RING, :].bitcast(fp32),
                                  ALU.subtract).then_inc(s_lo2, 1)
                if I == J and h == UPB - 1:
                    finish(fin)
                    fin += 1

        @block.tensor
        def _(eng):
            def mm(bank_, w, v, start=False, stop=True):
                return eng.matmul(bank_, w, v, start=start, stop=stop, skip_group_check=True)

            eng.sem_inc(s_free, RING)
            for count in (s_evac, s_ep, s_ep_out, c_used):
                eng.sem_inc(count, 1)
            eng.wait_ge(s_setup_d, 8 * 16)
            mm(EA[0][:, 0:3 * H + 2], w_gat_t[:, :], gat[:, :], start=True).then_inc(s_w, 1)
            eng.wait_ge(s_wsplit, 10)
            eng.wait_ge(s_const, 5)
            with eng.Fori(0, BLOCKS) as I:
                for u in range(UNITS):
                    g = UNITS * I + u
                    J = u // UPB
                    s = u % RING
                    if u == 0:
                        eng.wait_ge(s_evac, 4 * I + 1)
                        eng.wait_ge(s_hi, g + 1)
                        mm(AX1[:, :], zero_w[:, :], hi[:, s, 0:BI], start=True)
                    eng.wait_ge(s_mask, g + 1)
                    for t in range(UT):
                        j = UT * u + t
                        v = slice(t * BI, (t + 1) * BI)
                        mm(PLUS[:, :], h_split[:, j, :], mask[:, s, v], start=(j == 0))
                        mm(COUNT[:, :], ones[:, :], mask[:, s, v], start=(j == 0))
                    eng.wait_ge(s_lo, g + 1)
                    if J < BLOCKS - 1:
                        with eng.If(I > J):
                            eng.wait_ge(s_x1, 2 * (J + 1))
                            for t in range(UT):
                                j = UT * u + t
                                v = slice(t * BI, (t + 1) * BI)
                                mm(AX1[:, :], x1_split[:, j, :], hi[:, s, v])
                                mm(AX1[:, :], x1_split[:, j, :], lo[:, s, v])
                    for t in range(UT):
                        j = UT * u + t
                        v = slice(t * BI, (t + 1) * BI)
                        mm(VALUE[:, :], h_split[:, j, :], hi[:, s, v], start=(j == 0))
                        last = mm(VALUE[:, :], h_split[:, j, :], lo[:, s, v])
                    last.then_inc(s_free, 1)
                eng.wait_ge(s_above, I + 1)
                eng.wait_ge(s_ep_out, 2 * CH * I + 1)
                eng.transpose(EB[0][0:1, 0:P], above_max[:, :], ident[:, :]).then_inc(s_above_t, 1)
                eng.wait_ge(s_flag, I + 1)
                seen(eng)
                flag = eng.value_load(has_minus[0:1, bass.ds(I, 1)])
                with eng.If(flag > 0):
                    for k in range(TILES):
                        eng.wait_ge(c_dve, 3 * (TILES * I + k + 1))
                        mm(EA[0][:, :], h_split[:, k, :], c_mask[:, :], start=(k == 0))
                        mm(EA[1][:, :], ones[:, :], c_mask[:, :], start=(k == 0))
                        mm(EB[1][:, :], h_split[:, k, :], c_hi[:, :], start=(k == 0))
                        mm(EB[1][:, :], h_split[:, k, :], c_lo[:, :]).then_inc(c_used, 1)
                with eng.Else():
                    eng.sem_inc(c_used, TILES)
                eng.wait_ge(c_out, 3 * (I + 1))
                eng.wait_ge(s_evac, 4 * (I + 1) + 1)
                eng.wait_ge(s_xt, I + 1)
                for c in range(CH):
                    cs = slice(c * P, (c + 1) * P)
                    A, B = EA[c % 2], EB[c % 2]
                    gate3 = A[:, 0:3 * P].rearrange("p (g n) -> p g n", g=3)[:, :, 0:H]
                    if c >= 2:
                        eng.wait_ge(s_ep_out, 2 * (CH * I + c - 1) + 1)
                    mm(A[:, :], ones[0:H, :], bias_split[:, :], start=True)
                    mm(A[:, :], xt_split[:, cs], w_h_hi[:, :])
                    mm(A[:, :], xt_split[:, cs], w_h_lo[:, :])
                    mm(gate3, plus_sb[:, cs], w_plus[:, :].rearrange("p (g f) -> p g f", g=3))
                    with eng.If(flag > 0):
                        mm(gate3, minus_sb[:, cs], w_minus[:, :].rearrange("p (g f) -> p g f", g=3))
                        mm(B[:, 196:196 + 3 * H], nvalue_sb[:, cs], w_value[:, :], start=True)
                        mm(B[:, 195:196], ncount_sb[:, cs], ident[0:1, 0:1], start=True)
                        mm(B[:, 192:194], minus_sb[:, cs], a_minus[:, :], start=True)
                        mm(B[:, 192:194], plus_sb[:, cs], a_plus[:, :])
                    with eng.Else():
                        mm(B[:, 192:194], plus_sb[:, cs], a_plus[:, :], start=True)
                    mm(B[:, 194:195], count_sb[:, cs], ident[0:1, 0:1], start=True)
                    mm(B[:, 0:3 * H], value_sb[:, cs], w_value[:, :], start=True).then_inc(s_ep, 1)

            eng.sem_inc(s_free2, RING)
            eng.wait_ge(s_ep_out, 2 * CH * BLOCKS + 1)
            eng.wait_ge(s_x1, 2 * BLOCKS)

            def finish(n):
                J = BLOCKS - 1 - n
                eng.wait_ge(s_ax_sb, n + 1)
                if n:
                    eng.wait_ge(s_fin_rd, n)
                for c in range(CH):
                    o = bank[BLOCKS - 1][:, c * H:(c + 1) * H]
                    mm(o, ax_part[:, J, c * P:(c + 1) * P], pair_ident[:, :], start=True)
                    last = mm(o, ax_sb[:, c * P:(c + 1) * P], pair_ident[:, :])
                last.then_inc(s_fin, 1)

            fin = 0
            for n, (J, I, h) in enumerate(UNITS2):
                s = n % RING
                eng.wait_ge(s_lo2, n + 1)
                for t in range(UT):
                    j = UT * (UPB * J + h) + t
                    v = slice(t * BI, (t + 1) * BI)
                    mm(bank[I][:, :], x1_split[:, j, :], hi[:, s, v], start=(J == BLOCKS - 1 and h == 0 and t == 0))
                    last = mm(bank[I][:, :], x1_split[:, j, :], lo[:, s, v])
                last.then_inc(s_free2, 1)
                if I == J and h == UPB - 1:
                    eng.wait_ge(s_free2, RING + n + 1)
                    eng.sem_inc(s_ax, 1)
                    finish(fin)
                    fin += 1


def kernel(x, adj, L0_gnn_W_gat, L0_gnn_a_gat, L0_gnn_w_ih_e, L0_gnn_w_hh_e, L0_gnn_b_ih_e,
           L0_gnn_b_hh_e, L0_gnn_w_ih_n, L0_gnn_w_hh_n, L0_gnn_b_ih_n, L0_gnn_b_hh_n, L1_gnn_t):
    import numpy as np
    import concourse.bacc as bacc
    from concourse.bass_utils import run_bass_kernel_spmd as run

    N, H = x.shape
    P, BI, UT = 128, 512, 2
    B = N // BI
    x, adj = np.asarray(x), np.asarray(adj)

    def gates(e, n, parts):
        e3, n3 = (np.asarray(a).T.reshape(-1, 3, H) for a in (e, n))
        full = np.zeros((e3.shape[0], 4, 2, H), np.float32)
        for third, part in enumerate(parts):
            full[:, part, 0] = e3[:, third]
            full[:, part, 1] = n3[:, third]
        return full.reshape(-1, 8 * H)

    w_ih_e = np.asarray(L0_gnn_w_ih_e).T
    w_h = gates(L0_gnn_w_hh_e, L0_gnn_w_hh_n, (0, 1, 3))
    b_hh = gates(np.asarray(L0_gnn_b_hh_e)[:, None], np.asarray(L0_gnn_b_hh_n)[:, None], (0, 1, 3))
    b_ih = gates(np.asarray(L0_gnn_b_ih_e)[:, None], np.asarray(L0_gnn_b_ih_n)[:, None], (0, 1, 2))
    bias = np.zeros((H, 8 * H), np.float32)
    bias[0:2] = bias[32:34] = np.concatenate([b_hh, b_ih])
    a = np.asarray(L0_gnn_a_gat).reshape(2, H).T
    w_gat_t = np.asarray(L0_gnn_W_gat).T
    xt = np.ascontiguousarray(x.T).reshape(H, B, BI).transpose(1, 0, 2)
    arrays = {
        "adj_t": adj.reshape(B, BI, N // (UT * P), UT, P).transpose(0, 2, 4, 3, 1),
        "x_rows_d": x.reshape(N // P, P, H).transpose(1, 0, 2),
        "x_t_d": np.concatenate([xt, xt], axis=1),
        "diag_d": np.diagonal(adj).reshape(N // P, P).T,
        "gat_d": np.concatenate([np.asarray(L0_gnn_w_ih_n).T, a], axis=1),
        "w_gat_t_d": np.concatenate([w_gat_t, w_gat_t], axis=1),
        "w_plus_d": np.concatenate([w_ih_e[:H], w_ih_e[:H]]),
        "w_minus_d": np.concatenate([w_ih_e[H:], w_ih_e[H:]]),
        "w_h_d": np.concatenate([w_h, w_h]),
        "bias_d": bias,
    }
    arrays = {name: np.ascontiguousarray(v) for name, v in arrays.items()}
    nc = bacc.Bacc("TRN2", target_bir_lowering=False, num_devices=1)
    args = [nc.dram_tensor(name, v.shape, mybir.dt.from_np(v.dtype), kind="ExternalInput").ap()
            for name, v in arrays.items()]
    out = nc.dram_tensor("out", (N, H), mybir.dt.float32, kind="ExternalOutput").ap()
    gnn_ode_kernel(nc, *args, out)
    return run(nc, [arrays], core_ids=[0]).results[0]["out"]
```

```python
import concourse.bass as bass
from concourse import mybir
from contextlib import ExitStack

NEG_INF = -9.0e15
ALPHA = 0.2
EPS = 1e-5
AWAY = 1.0 + 2.0 ** -12


def gnn_ode_kernel(nc: bass.Bass, adj_t, x_rows_d, x_t_d, diag_d, gat_d, w_gat_t_d, w_plus_d,
                   w_minus_d, w_h_d, bias_d, out):
    fp32, f32r, i32 = mybir.dt.float32, mybir.dt.float32r, mybir.dt.int32
    ALU, ACT, AX = mybir.AluOpType, mybir.ActivationFunctionType, mybir.AxisListType

    BLOCKS, UNITS, P, UT, BI = adj_t.shape
    N = BLOCKS * BI
    TILES = N // P
    CH = BI // P
    UPB = UNITS // BLOCKS
    H = 64
    UW = UT * BI
    RAW = 8
    RING = 4
    LATE_J = -1

    ctx = ExitStack()
    with ctx:
        def sb(name, shape, dt=fp32):
            return ctx.enter_context(nc.sbuf_tensor(name, shape, dt))

        def sem(name):
            return ctx.enter_context(nc.semaphore(name))

        raw = sb("raw", [P, RAW, UW])
        mask = sb("mask", [P, RING, UW], f32r)
        hi = sb("hi", [P, RING, UW], f32r)
        lo = sb("lo", [P, RING, UW], f32r)
        h_split = sb("h_split", [P, TILES, 2 * H], f32r)
        x1_split = sb("x1_split", [P, TILES, 2 * H], f32r)
        x_rows = sb("x_rows", [P, TILES, H])
        x1_rows = sb("x1_rows", [P, TILES, H])
        ax_part = sb("ax_part", [P, BLOCKS, BI])
        diag = sb("diag", [P, TILES])
        xt_raw = sb("xt_raw", [P, BI])
        xt_split = sb("xt_split", [P, BI], f32r)
        ones = sb("ones", [P, P], f32r)
        ident = sb("ident", [P, P])
        pair_ident = sb("pair_ident", [P, H])
        zero_w = sb("zero_w", [P, P], f32r)
        gat = sb("gat", [H, 3 * H + 2])
        w_gat_t = sb("w_gat_t", [H, 2 * H])
        w_plus = sb("w_plus", [P, 3 * H])
        w_minus = sb("w_minus", [P, 3 * H])
        w_value = sb("w_value", [P, 3 * H])
        a_plus = sb("a_plus", [P, 2])
        a_minus = sb("a_minus", [P, 2])
        w_h_raw = sb("w_h_raw", [P, 4 * P])
        w_h_hi = sb("w_h_hi", [P, 4 * P], f32r)
        w_h_lo = sb("w_h_lo", [P, 4 * P], f32r)
        bias_raw = sb("bias_raw", [H, 4 * P])
        bias_split = sb("bias_split", [H, 4 * P], f32r)
        plus_sb = sb("plus_sb", [P, BI])
        value_sb = sb("value_sb", [P, BI])
        count_sb = sb("count_sb", [1, BI])
        minus_sb = sb("minus_sb", [P, BI])
        nvalue_sb = sb("nvalue_sb", [P, BI])
        ncount_sb = sb("ncount_sb", [1, BI])
        gates = sb("gates", [P, CH, 4, P])
        vals = sb("vals", [P, CH, 388])
        above = sb("above", [P, UNITS])
        above_max = sb("above_max", [P, 1])
        above_all = sb("above_all", [1, 1])
        has_minus = sb("has_minus", [1, BLOCKS], i32)
        leaky = sb("leaky", [P, CH, 2])
        absent = sb("absent", [P, CH, 2])
        top = sb("top", [P, CH, 1])
        expo = sb("expo", [P, CH, 3])
        cnt = sb("cnt", [P, CH, 3])
        norm = sb("norm", [P, CH, 1])
        att = sb("att", [P, CH, 3])
        y = sb("y", [P, CH, H])
        sq = sb("sq", [P, CH, H])
        mean = sb("mean", [P, CH, 1])
        stats = sb("stats", [P, CH, 6])
        moments = sb("moments", [P, CH, 2])
        mix = sb("mix", [P, CH, 2, H])
        ode = sb("ode", [P, CH, H])
        var = sb("var", [P, CH, 1])
        rstd = sb("rstd", [P, CH, 1])
        neg_half = sb("neg_half", [P, CH, 1])
        ax_sb = sb("ax_sb", [P, BI])
        res = sb("res", [P, 2, CH, H])
        c_raw = gates[:, 0:1].rearrange("p a b c -> p (a b c)")
        c_mask = sb("c_mask", [P, BI], f32r)
        c_hi = sb("c_hi", [P, BI], f32r)
        c_lo = sb("c_lo", [P, BI], f32r)

        bank = [ctx.enter_context(nc.psum_tensor(f"bank{n}", [P, BI], fp32)) for n in range(8)]
        PLUS, COUNT, VALUE, AX1 = bank[0:4]
        EA, EB = bank[4:6], bank[6:8]

        s_raw = [sem(f"s_raw{n}") for n in range(RAW)]
        s_x_first = sem("s_x_first")
        s_x_rest = sem("s_x_rest")
        s_h_first = sem("s_h_first")
        s_h_rest = sem("s_h_rest")
        s_setup_d = sem("s_setup_d")
        s_const = sem("s_const")
        s_w = sem("s_w")
        s_wsplit = sem("s_wsplit")
        s_diag = sem("s_diag")
        s_tile = sem("s_tile")
        s_mask = sem("s_mask")
        s_hi = sem("s_hi")
        s_lo = sem("s_lo")
        s_free = sem("s_free")
        s_evac = sem("s_evac")
        s_above = sem("s_above")
        s_above_t = sem("s_above_t")
        s_flag = sem("s_flag")
        s_seen = sem("s_seen")
        s_xt_d = sem("s_xt_d")
        s_xt = sem("s_xt")
        s_ep = sem("s_ep")
        s_ep_out = sem("s_ep_out")
        s_expo = sem("s_expo")
        s_exp = sem("s_exp")
        s_gin = sem("s_gin")
        s_act = sem("s_act")
        s_nin = sem("s_nin")
        s_y = sem("s_y")
        s_ode = sem("s_ode")
        s_x1r = sem("s_x1r")
        s_var = sem("s_var")
        s_rstd = sem("s_rstd")
        s_x1 = sem("s_x1")
        s_xt_hi = sem("s_xt_hi")
        s_dve = sem("s_dve")
        s_dve2 = sem("s_dve2")
        s_pool = sem("s_pool")
        c_dma = sem("c_dma")
        c_diag = sem("c_diag")
        c_tile = sem("c_tile")
        c_dve = sem("c_dve")
        c_gin = sem("c_gin")
        c_used = sem("c_used")
        c_out = sem("c_out")
        s_hi2 = sem("s_hi2")
        s_lo2 = sem("s_lo2")
        s_ax_sb = sem("s_ax_sb")
        s_fin = sem("s_fin")
        s_fin_rd = sem("s_fin_rd")
        s_res = sem("s_res")
        s_out = [sem(f"s_out{n}") for n in range(2)]

        def unit_at(q):
            return UPB * (BLOCKS - 1 - q // UPB) + q % UPB

        def lag(J):
            return 1 if J > LATE_J else 0

        UNITS2 = [(I, J, h) for I in range(BLOCKS) for J in range(BLOCKS) if I <= J + lag(J)
                  for h in range(UPB)]
        LAST2 = {I: max(n for n, x in enumerate(UNITS2) if x[0] == I) for I in range(BLOCKS)}
        END2 = len(UNITS2) - 1
        LOADS1 = BLOCKS * UNITS
        FIRST = TILES - CH

        def ended(n, behind):
            return [I for I in range(BLOCKS)
                    if LAST2[I] + behind == n or (n == END2 and LAST2[I] + behind > n)]

        PE_ABOVE, PE_FLAG, PE_CHUNKS = 1, 3, 4
        DVE_FLAG, DVE_EXPO, DVE_ATT, DVE_N, DVE_NORM, DVE_X1 = 3, 8, 9, 10, 14, 15
        ACT_SUMS, ACT_FLAG, ACT_CHUNKS, ACT_EXP, ACT_RZ, ACT_N = 2, 5, 6, 9, 10, 11
        POOL_FIX, POOL_Y, POOL_POWER = 7, 14, 15

        block = ctx.enter_context(nc.Block())

        def seen(eng):
            eng.sem_inc(s_seen, 1)

        def bc(ap, n):
            return ap.to_broadcast([P, CH, n])

        def load_flag(eng, K):
            eng.wait_ge(s_flag, K + 1)
            seen(eng)
            return eng.value_load(has_minus[0:1, bass.ds(K, 1)])

        @block.sync
        def _(eng):
            def load(slot, src):
                eng.dma_start(raw[:, slot, :], src.rearrange("p t i -> p (t i)")).then_inc(s_raw[slot], 16)

            eng.dma_start(x_rows[:, FIRST:, :], x_rows_d[:, FIRST:, :]).then_inc(s_x_first, 16)
            for q in range(UPB):
                load(q, adj_t[0, unit_at(q), :, :, :])
            eng.dma_start(x_rows[:, :FIRST, :], x_rows_d[:, :FIRST, :]).then_inc(s_x_rest, 16)
            for q in range(UPB, RAW):
                load(q, adj_t[0, unit_at(q), :, :, :])
            with eng.Fori(0, BLOCKS - 1) as I:
                for q in range(UNITS):
                    eng.wait_ge(s_lo, UNITS * I + q + 1)
                    seen(eng)
                    n = q + RAW
                    if n < UNITS:
                        load(n % RAW, adj_t[I, unit_at(n), :, :, :])
                    else:
                        load(n % RAW, adj_t[I + 1, unit_at(n - UNITS), :, :, :])
            for q in range(UNITS - RAW):
                eng.wait_ge(s_lo, UNITS * (BLOCKS - 1) + q + 1)
                load(q % RAW, adj_t[BLOCKS - 1, unit_at(q + RAW), :, :, :])
            for n, (I, J, h) in enumerate(UNITS2):
                if n < RAW:
                    eng.wait_ge(s_lo, LOADS1 - RAW + n + 1)
                else:
                    eng.wait_ge(s_lo2, n - RAW + 1)
                load(n % RAW, adj_t[I, UPB * J + h, :, :, :])

        @block.gpsimd
        def _(eng):
            eng.memset(ident[:, :], 0.0).then_inc(s_pool, 1)
            eng.memset(pair_ident[:, :], 0.0).then_inc(s_pool, 1)
            eng.memset(neg_half[:, :, :], -0.5).then_inc(s_const, 1)
            eng.wait_ge(s_pool, 2)
            eng.affine_select(out=ident[:, :], in_=ident[:, :], compare_op=ALU.not_equal, fill=1.0,
                              base=0, pattern=[[-1, P]], channel_multiplier=1).then_inc(s_const, 1)
            eng.affine_select(out=pair_ident[:, :], in_=pair_ident[:, :], compare_op=ALU.not_equal,
                              fill=1.0, base=0, pattern=[[-1, H]], channel_multiplier=1).then_inc(s_pool, 1)
            eng.wait_ge(s_pool, 3)
            eng.affine_select(out=pair_ident[:, :], in_=pair_ident[:, :], compare_op=ALU.not_equal,
                              fill=1.0, base=-H, pattern=[[-1, H]], channel_multiplier=1).then_inc(s_const, 1)
            POOL0, POOL_PER = 3, 6
            links = [0]

            def link(ins, K):
                links[0] += 1
                ins.then_inc(s_pool, 1)
                eng.wait_ge(s_pool, POOL_PER * K + POOL0 + links[0])

            def zero_diagonal(ap, q, s):
                part = ap[:, q * P:(q + 1) * P]
                eng.affine_select(out=part, in_=part, compare_op=ALU.not_equal, fill=0.0, base=0,
                                  pattern=[[-1, P]], channel_multiplier=1).then_inc(s, 1)

            def power():
                eng.tensor_tensor(rstd[:, :, :], var[:, :, :], neg_half[:, :, :], ALU.pow).then_inc(s_rstd, 1)

            def last_steps(q, K):
                if q == POOL_FIX:
                    links[0] = 0
                    flag = load_flag(eng, K)
                    with eng.If(flag > 0):
                        for J in range(BLOCKS):
                            for t in range(CH):
                                eng.wait_ge(c_dma, 16 * (TILES * K + CH * J + t + 1))
                                seen(eng)
                                with eng.If(K == J):
                                    zero_diagonal(c_raw, t, c_diag)
                                    eng.wait_ge(c_diag, CH * K + t + 1)
                                eng.sem_inc(c_tile, 1)
                    with eng.Else():
                        eng.sem_inc(c_tile, TILES)
                        eng.sem_inc(c_diag, CH)
                if q == POOL_Y:
                    eng.wait_ge(s_act, 3 * K + 3)
                    seen(eng)
                    xb = x_rows[:, bass.ds(CH * K, CH), :]
                    n_out = gates[:, :, 2, :].rearrange("p c (e f) -> p c e f", e=2)
                    z = gates[:, :, 1, :].rearrange("p c (e f) -> p c e f", e=2)
                    link(eng.tensor_tensor(mix[:, :, 0, :], xb, n_out[:, :, 0, :], ALU.subtract), K)
                    seen(eng)
                    link(eng.tensor_tensor(mix[:, :, 1, :], xb, n_out[:, :, 1, :], ALU.subtract), K)
                    link(eng.tensor_tensor(mix[:, :, :, :], mix[:, :, :, :], z, ALU.mult), K)
                    link(eng.tensor_tensor(mix[:, :, :, :], mix[:, :, :, :], n_out, ALU.add), K)
                    link(eng.tensor_tensor(y[:, :, :], mix[:, :, 0, :], mix[:, :, 1, :], ALU.add), K)
                    seen(eng)
                    link(eng.tensor_tensor(y[:, :, :], y[:, :, :],
                                           bc(diag[:, bass.ds(CH * K, CH)].rearrange("p (c o) -> p c o", o=1), H),
                                           ALU.mult), K)
                    seen(eng)
                    eng.tensor_tensor(y[:, :, :], y[:, :, :], xb, ALU.add).then_inc(s_y, 1)
                if q == POOL_POWER:
                    eng.wait_ge(s_var, K + 1)
                    power()
                    assert links[0] == POOL_PER, links[0]

            def one_block(I, K):
                for q in range(UNITS):
                    J, h = unit_at(q) // UPB, unit_at(q) % UPB
                    eng.wait_ge(s_raw[q % RAW], 16 * ((UNITS // RAW) * I + q // RAW + 1))
                    seen(eng)

                    def own_columns():
                        for t in range(UT):
                            zero_diagonal(raw[:, q % RAW, t * BI:(t + 1) * BI], UT * h + t, s_diag)
                        eng.wait_ge(s_diag, CH * I + UT * (h + 1))

                    if K is None:
                        if J == I:
                            own_columns()
                    else:
                        with eng.If(I == J):
                            own_columns()
                    eng.sem_inc(s_tile, 1)
                    if q == 7:
                        eng.dma_start(xt_raw[:, :], x_t_d[I]).then_inc(s_xt_d, 16)
                    if K is not None:
                        last_steps(q, K)
                if K is not None:
                    eng.wait_ge(s_rstd, K + 1)
                eng.wait_ge(s_xt_hi, I + 1)
                eng.tensor_tensor(xt_split[H:P, :], xt_raw[H:P, :], xt_split[H:P, :].bitcast(fp32),
                                  ALU.subtract).then_inc(s_xt, 1)
                eng.wait_ge(s_xt, I + 1)

            one_block(0, None)
            eng.wait_ge(s_setup_d, 7 * 16)
            with eng.Fori(1, BLOCKS) as I:
                one_block(I, I - 1)
            for q in range(UNITS):
                last_steps(q, BLOCKS - 1)
            for n in range(BLOCKS):
                x1b = x1_rows[:, CH * n:CH * (n + 1), :]
                if n:
                    eng.wait_ge(s_y, BLOCKS + n)
                else:
                    eng.wait_ge(s_x1r, CH * BLOCKS)
                eng.tensor_scalar(ode[:, :, :], x1b, -0.1, 1.0, ALU.mult, ALU.add).then_inc(s_ode, 1)
                eng.wait_ge(s_ode, 2 * n + 1)
                eng.tensor_tensor(ode[:, :, :], ode[:, :, :], x1b, ALU.add).then_inc(s_ode, 1)
                eng.wait_ge(s_ode, 2 * n + 2)
                eng.wait_ge(s_var, BLOCKS + n + 1)
                power()
                eng.wait_ge(s_res, CH * (n + 1))
                eng.dma_start(out[n * BI:(n + 1) * BI, :].rearrange("(c p) f -> p c f", p=P),
                              res[:, n % 2, :, :]).then_inc(s_out[n % 2], 16)
            for done in s_out:
                eng.wait_ge(done, 16 * BLOCKS // 2)

        @block.scalar
        def _(eng):
            eng.wait_ge(s_x_first, 16)
            eng.activation(h_split[:, FIRST:, 0:H], x_rows[:, FIRST:, :], ACT.Copy).then_inc(s_h_first, 1)

            def first_steps(q):
                if q == 0:
                    eng.wait_ge(s_x_rest, 16)
                    eng.activation(h_split[:, :FIRST, 0:H], x_rows[:, :FIRST, :], ACT.Copy).then_inc(s_h_rest, 1)
                if q == 2:
                    eng.dma_start(gat[:, :], gat_d).then_inc(s_setup_d, 16)
                    eng.dma_start(w_gat_t[:, :], w_gat_t_d).then_inc(s_setup_d, 16)
                    eng.dma_start(w_plus[:, :], w_plus_d).then_inc(s_setup_d, 16)
                    eng.dma_start(w_minus[:, :], w_minus_d).then_inc(s_setup_d, 16)
                    eng.dma_start(w_h_raw[:, :], w_h_d).then_inc(s_setup_d, 16)
                    eng.dma_start(bias_raw[:, :], bias_d).then_inc(s_setup_d, 16)
                    eng.dma_start(diag[:, :], diag_d).then_inc(s_setup_d, 16)
                if q == 8:
                    eng.wait_ge(s_setup_d, 7 * 16)
                    eng.activation(w_h_hi[:, :], w_h_raw[:, :], ACT.Copy).then_inc(s_wsplit, 1)

            def copy_chunk(c, K, flag):
                eng.wait_ge(s_ep, CH * K + c + 2)
                eng.activation(gates[:, c, :, :].rearrange("p g n -> p (g n)"), EA[c % 2][:, :],
                               ACT.Copy).then_inc(s_ep_out, 1)
                with eng.If(flag > 0):
                    eng.activation(vals[:, c, :], EB[c % 2][:, 0:388], ACT.Copy).then_inc(s_ep_out, 1)
                with eng.Else():
                    eng.activation(vals[:, c, 0:195], EB[c % 2][:, 0:195], ACT.Copy).then_inc(s_ep_out, 1)

            def last_steps(q, K, flag):
                if q == ACT_SUMS:
                    eng.wait_ge(s_free, UNITS * (K + 1) + RING)
                    eng.activation(plus_sb[:, :], PLUS[:, :], ACT.Copy).then_inc(s_evac, 1)
                    eng.activation(count_sb[:, :], COUNT[0:1, :], ACT.Copy).then_inc(s_evac, 1)
                    eng.activation(value_sb[:, :], VALUE[:, :], ACT.Copy).then_inc(s_evac, 1)
                    eng.activation(ax_part[:, bass.ds(K, 1), :].rearrange("p a i -> p (a i)"), AX1[:, :],
                                   ACT.Copy).then_inc(s_evac, 1)
                if q == ACT_FLAG:
                    flag = load_flag(eng, K)
                    with eng.If(flag > 0):
                        with eng.Fori(0, UNITS) as u:
                            for t in range(UT):
                                eng.wait_ge(c_used, TILES * K + UT * u + t + 1)
                                eng.dma_start(c_raw, adj_t[K, u, :, t, :]).then_inc(c_dma, 16)
                    with eng.Else():
                        eng.sem_inc(c_dma, 16 * TILES)
                if q == ACT_CHUNKS:
                    copy_chunk(0, K, flag)
                    copy_chunk(1, K, flag)
                if q == ACT_CHUNKS + 1:
                    copy_chunk(2, K, flag)
                    copy_chunk(3, K, flag)
                if q == ACT_EXP:
                    eng.wait_ge(s_expo, 2 * K + 2)
                    eng.activation(expo[:, :, :], expo[:, :, :], ACT.Exp).then_inc(s_exp, 1)
                if q == ACT_RZ:
                    eng.wait_ge(s_gin, K + 1)
                    eng.activation(gates[:, :, 0:2, :], gates[:, :, 0:2, :], ACT.Tanh,
                                   scale=0.5).then_inc(s_act, 1)
                    eng.wait_ge(s_act, 3 * K + 1)
                    eng.activation(gates[:, :, 1, :], gates[:, :, 1, :], ACT.Copy, bias=0.5,
                                   scale=0.5).then_inc(s_act, 1)
                if q == ACT_N:
                    eng.wait_ge(s_nin, K + 1)
                    eng.activation(gates[:, :, 2, :], gates[:, :, 2, :], ACT.Tanh).then_inc(s_act, 1)
                return flag

            def one_block(I, K):
                flag = None
                for q in range(UNITS):
                    g = UNITS * I + q
                    eng.wait_ge(s_tile, g + 1)
                    eng.wait_ge(s_free, g + 1)
                    eng.activation(hi[:, q % RING, :], raw[:, q % RAW, :], ACT.Copy,
                                   scale=AWAY).then_inc(s_hi, 1)
                    if K is not None:
                        flag = last_steps(q, K, flag)
                    else:
                        first_steps(q)
                    if q == 11:
                        eng.wait_ge(s_xt_d, 16 * (I + 1))
                        eng.wait_ge(s_ep, CH * I + 1)
                        eng.activation(xt_split[:, :], xt_raw[:, :], ACT.Copy).then_inc(s_xt_hi, 1)

            one_block(0, None)
            with eng.Fori(1, BLOCKS) as I:
                one_block(I, I - 1)
            flag = None
            for n, (I, J, h) in enumerate(UNITS2):
                eng.wait_ge(s_raw[n % RAW], 16 * (LOADS1 // RAW + n // RAW + 1))
                eng.wait_ge(s_free, LOADS1 + n + 1)
                eng.activation(hi[:, n % RING, :], raw[:, n % RAW, :], ACT.Copy).then_inc(s_hi2, 1)
                flag = last_steps(n, BLOCKS - 1, flag)
                for F in ended(n, 2):
                    eng.wait_ge(s_free, LOADS1 + RING + LAST2[F] + 1)
                    if F:
                        eng.wait_ge(s_fin, F)
                    eng.activation(ax_sb[:, :], bank[F % 2][:, :], ACT.Copy).then_inc(s_ax_sb, 1)

        @block.vector
        def _(eng):
            eng.memset(mask[:, 0, 0:P].bitcast(fp32), 1.0).then_inc(s_dve, 1)
            eng.memset(zero_w[:, :].bitcast(fp32), 0.0).then_inc(s_const, 1)
            eng.memset(bias_split[:, :].bitcast(fp32), 0.0).then_inc(s_dve, 1)
            eng.wait_ge(s_dve, 2)
            eng.tensor_copy(ones[:, :], mask[:, 0, 0:P].bitcast(fp32)).then_inc(s_const, 1)
            eng.wait_ge(s_const, 5)
            eng.wait_ge(s_h_first, 1)
            eng.tensor_tensor(h_split[:, FIRST:, H:2 * H], x_rows[:, FIRST:, :],
                              h_split[:, FIRST:, 0:H].bitcast(fp32), ALU.subtract).then_inc(s_h_first, 1)

            def first_steps(q):
                if q == 0:
                    eng.wait_ge(s_h_rest, 1)
                    eng.tensor_tensor(h_split[:, :FIRST, H:2 * H], x_rows[:, :FIRST, :],
                                      h_split[:, :FIRST, 0:H].bitcast(fp32), ALU.subtract).then_inc(s_h_rest, 1)
                if q == 9:
                    eng.wait_ge(s_wsplit, 1)
                    eng.tensor_tensor(w_h_lo[:, :], w_h_raw[:, :], w_h_hi[:, :].bitcast(fp32),
                                      ALU.subtract).then_inc(s_wsplit, 1)
                    eng.tensor_copy(bias_split[0:2, :], bias_raw[0:2, :]).then_inc(s_wsplit, 1)
                    eng.tensor_copy(bias_split[32:34, :], bias_raw[32:34, :]).then_inc(s_dve, 1)
                    eng.wait_ge(s_dve, 3)
                    eng.tensor_tensor(bias_split[32:34, :], bias_raw[32:34, :],
                                      bias_split[32:34, :].bitcast(fp32), ALU.subtract).then_inc(s_wsplit, 1)
                if q == 14:
                    eng.wait_ge(s_w, 1)
                    eng.tensor_copy(w_value[:, :], EA[0][:, 0:3 * H]).then_inc(s_wsplit, 1)
                    eng.tensor_copy(a_plus[:, :], EA[0][:, 3 * H:3 * H + 2]).then_inc(s_wsplit, 1)
                    eng.tensor_copy(a_minus[:, 0:1], EA[0][:, 3 * H + 1:3 * H + 2]).then_inc(s_wsplit, 1)
                    eng.tensor_copy(a_minus[:, 1:2], EA[0][:, 3 * H:3 * H + 1]).then_inc(s_wsplit, 1)

            BASE = 3
            PER_BLOCK = 27
            links = [0]
            links2 = [0]

            def mark(ins):
                links[0] += 1
                ins.then_inc(s_dve, 1)

            def join(K):
                eng.wait_ge(s_dve, PER_BLOCK * K + BASE + links[0])

            def link(ins, K):
                mark(ins)
                join(K)

            def mark2(ins):
                links2[0] += 1
                ins.then_inc(s_dve2, 1)

            def join2(K=None):
                eng.wait_ge(s_dve2, links2[0])

            def moments_of_y(mark, join, K):
                for c in range(CH):
                    mark(eng.bn_stats(stats[:, c, :], y[:, c, :]))
                join(K)
                seen(eng)
                for c in range(CH):
                    mark(eng.bn_aggr(moments[:, c, :], stats[:, c, :]))
                join(K)
                eng.tensor_scalar(var[:, :, :], moments[:, :, 1:2], EPS, None, ALU.add).then_inc(s_var, 1)

            def normalised(o, c):
                return eng.tensor_scalar(o, y[:, c, :], moments[:, c, 0:1], rstd[:, c, :],
                                         ALU.subtract, ALU.mult)

            def correct(K):
                with eng.Fori(0, TILES) as k:
                    n = TILES * K + k
                    eng.wait_ge(c_tile, n + 1)
                    eng.wait_ge(c_used, n + 1)
                    eng.tensor_scalar(c_mask[:, :], c_raw, 0.0, None, ALU.is_lt).then_inc(c_dve, 1)
                    eng.tensor_scalar(c_hi[:, :], c_raw, 0.0, None, ALU.min).then_inc(c_dve, 1)
                    eng.wait_ge(c_dve, 3 * n + 2)
                    eng.scalar_tensor_tensor(c_lo[:, :], c_raw, 0.0, c_hi[:, :].bitcast(fp32),
                                             ALU.min, ALU.subtract).then_inc(c_dve, 1)
                eng.wait_ge(c_used, TILES * (K + 1) + 1)
                eng.tensor_copy(minus_sb[:, :], EA[0][:, :]).then_inc(c_out, 1)
                eng.tensor_copy(ncount_sb[:, :], EA[1][0:1, :]).then_inc(c_out, 1)
                eng.tensor_copy(nvalue_sb[:, :], EB[1][:, :]).then_inc(c_out, 1)

            def last_steps(q, K, flag):
                if q == DVE_FLAG:
                    eng.wait_ge(s_above_t, K + 1)
                    links[0] = 0
                    link(eng.reduce_max(above_all[:, :], EB[0][0:1, 0:P], AX.X), K)
                    eng.tensor_scalar(has_minus[0:1, bass.ds(K, 1)], above_all[:, :], 0.0, None,
                                      ALU.is_gt).then_inc(s_flag, 1)
                    flag = load_flag(eng, K)
                    with eng.If(flag > 0):
                        correct(K)
                    with eng.Else():
                        eng.sem_inc(c_dve, 3 * TILES)
                        eng.sem_inc(c_out, 3)
                if q == DVE_EXPO:
                    eng.wait_ge(s_ep_out, 2 * CH * (K + 1) + 1)
                    seen(eng)
                    with eng.If(flag > 0):
                        eng.tensor_copy(cnt[:, :, 1:2], vals[:, :, 195:196]).then_inc(s_dve, 1)
                    with eng.Else():
                        eng.memset(cnt[:, :, 1:2], 0.0).then_inc(s_dve, 1)
                    links[0] += 1
                    mark(eng.tensor_copy(cnt[:, :, 0:1], vals[:, :, 194:195]))
                    mark(eng.scalar_tensor_tensor(leaky[:, :, :], vals[:, :, 192:194], ALPHA, vals[:, :, 192:194],
                                                  ALU.mult, ALU.max))
                    join(K)
                    mark(eng.tensor_scalar(absent[:, :, :], cnt[:, :, 0:2], 0.0, 4 * NEG_INF, ALU.is_le, ALU.mult))
                    mark(eng.tensor_tensor(cnt[:, :, 2:3], cnt[:, :, 0:1], cnt[:, :, 1:2], ALU.add))
                    join(K)
                    mark(eng.tensor_tensor(leaky[:, :, :], leaky[:, :, :], absent[:, :, :], ALU.add))
                    mark(eng.tensor_scalar(cnt[:, :, 2:3], cnt[:, :, 2:3], -1.0, float(N), ALU.mult, ALU.add))
                    join(K)
                    mark(eng.scalar_tensor_tensor(top[:, :, :], leaky[:, :, 0:1], NEG_INF, leaky[:, :, 1:2],
                                                  ALU.max, ALU.max))
                    join(K)
                    eng.tensor_tensor(expo[:, :, 0:2], leaky[:, :, :], bc(top[:, :, :], 2),
                                      ALU.subtract).then_inc(s_expo, 1)
                    eng.tensor_scalar(expo[:, :, 2:3], top[:, :, :], -1.0, NEG_INF, ALU.mult, ALU.add).then_inc(s_expo, 1)
                if q == DVE_ATT:
                    eng.wait_ge(s_exp, K + 1)
                    link(eng.tensor_tensor(cnt[:, :, :], cnt[:, :, :], expo[:, :, :], ALU.mult), K)
                    link(eng.reduce_sum(norm[:, :, :], cnt[:, :, :], AX.X), K)
                    link(eng.reciprocal(norm[:, :, :], norm[:, :, :]), K)
                    link(eng.tensor_tensor(att[:, :, 0:2], expo[:, :, 0:2], bc(norm[:, :, :], 2), ALU.mult), K)
                    mark(eng.tensor_tensor(att[:, :, 2:3], att[:, :, 1:2], att[:, :, 0:1], ALU.subtract))
                    for c in range(CH):
                        g3 = gates[:, c, 0:3, H:P]
                        v3 = vals[:, c, 0:3 * H].rearrange("p (g f) -> p g f", g=3)
                        mark(eng.scalar_tensor_tensor(g3, v3, att[:, c, 0:1], g3, ALU.mult, ALU.add))
                    join(K)
                    seen(eng)
                    with eng.If(flag > 0):
                        for c in range(CH):
                            g3 = gates[:, c, 0:3, H:P]
                            v3 = vals[:, c, 196:196 + 3 * H].rearrange("p (g f) -> p g f", g=3)
                            eng.scalar_tensor_tensor(g3, v3, att[:, c, 2:3], g3, ALU.mult, ALU.add).then_inc(c_gin, 1)
                    with eng.Else():
                        eng.sem_inc(c_gin, CH)
                    eng.wait_ge(c_gin, CH * (K + 1))
                    eng.sem_inc(s_gin, 1)
                if q == DVE_N:
                    eng.wait_ge(s_act, 3 * K + 1)
                    link(eng.scalar_tensor_tensor(gates[:, :, 3, :], gates[:, :, 0, :], 1.0, gates[:, :, 3, :],
                                                  ALU.add, ALU.mult), K)
                    eng.scalar_tensor_tensor(gates[:, :, 2, :], gates[:, :, 3, :], 0.5, gates[:, :, 2, :],
                                             ALU.mult, ALU.add).then_inc(s_nin, 1)
                if q == DVE_NORM:
                    eng.wait_ge(s_y, K + 1)
                    moments_of_y(mark, join, K)
                if q == DVE_X1:
                    eng.wait_ge(s_rstd, K + 1)
                    for c in range(CH):
                        normalised(x1_rows[:, bass.ds(CH * K + c, 1), :].rearrange("p a f -> p (a f)"),
                                   c).then_inc(s_x1r, 1)
                    eng.wait_ge(s_x1r, CH * (K + 1))
                    x1b = x1_rows[:, bass.ds(CH * K, CH), :]
                    x1h = x1_split[:, bass.ds(CH * K, CH), 0:H]
                    eng.tensor_copy(x1h, x1b).then_inc(s_x1, 1)
                    eng.wait_ge(s_x1, 2 * K + 1)
                    eng.tensor_tensor(x1_split[:, bass.ds(CH * K, CH), H:2 * H], x1b, x1h.bitcast(fp32),
                                      ALU.subtract).then_inc(s_x1, 1)
                    assert links[0] == PER_BLOCK, links[0]
                return flag

            def one_block(I, K):
                flag = None
                for q in range(UNITS):
                    g = UNITS * I + q
                    eng.wait_ge(s_tile, g + 1)
                    eng.wait_ge(s_free, g + 1)
                    eng.wait_ge(s_hi, g + 1)
                    eng.tensor_scalar(mask[:, q % RING, :], raw[:, q % RAW, :], 0.0, None,
                                      ALU.is_gt).then_inc(s_mask, 1)
                    eng.tensor_tensor_reduce(out=lo[:, q % RING, :], in0=raw[:, q % RAW, :],
                                             in1=hi[:, q % RING, :].bitcast(fp32), scale=1.0, scalar=-3.0e38,
                                             op0=ALU.subtract, op1=ALU.max,
                                             accum_out=above[:, q:q + 1]).then_inc(s_lo, 1)
                    if K is not None:
                        flag = last_steps(q, K, flag)
                    else:
                        first_steps(q)
                eng.wait_ge(s_lo, UNITS * (I + 1))
                eng.reduce_max(above_max[:, :], above[:, :], AX.X).then_inc(s_above, 1)
                eng.wait_ge(s_above, I + 1)

            one_block(0, None)
            with eng.Fori(1, BLOCKS) as I:
                one_block(I, I - 1)

            def finish(F):
                x1b = x1_rows[:, CH * F:CH * (F + 1), :]
                eng.wait_ge(s_fin, F + 1)
                axp = bank[2 + F % 2][:, 0:CH * H].rearrange("p (c f) -> p c f", c=CH)
                eng.tensor_tensor(sq[:, :, :], axp, x1b, ALU.mult).then_inc(s_fin_rd, 1)
                eng.wait_ge(s_fin_rd, F + 1)
                mark2(eng.reduce_sum(mean[:, :, :], sq[:, :, :], AX.X))
                join2()
                mark2(eng.tensor_scalar(mean[:, :, :], mean[:, :, :], 0.01, None, ALU.mult))
                join2()
                eng.wait_ge(s_ode, 2 * F + 2)
                for c in range(CH):
                    ins = eng.tensor_scalar(y[:, c, :], ode[:, c, :], mean[:, c, :], None, ALU.subtract)
                    if c == CH - 1:
                        ins.then_inc(s_y, 1)
                    else:
                        mark2(ins)
                eng.wait_ge(s_y, BLOCKS + F + 1)
                join2()
                moments_of_y(mark2, join2, None)
                eng.wait_ge(s_rstd, BLOCKS + F + 1)
                if F >= 2:
                    eng.wait_ge(s_out[F % 2], 16 * (F // 2))
                for c in range(CH):
                    normalised(res[:, F % 2, c, :], c).then_inc(s_res, 1)

            flag = None
            for n, (I, J, h) in enumerate(UNITS2):
                eng.wait_ge(s_hi2, n + 1)
                eng.tensor_tensor(lo[:, n % RING, :], raw[:, n % RAW, :], hi[:, n % RING, :].bitcast(fp32),
                                  ALU.subtract).then_inc(s_lo2, 1)
                flag = last_steps(n, BLOCKS - 1, flag)
                for F in ended(n, 4):
                    finish(F)

        @block.tensor
        def _(eng):
            def mm(o, w, v, start=False, stop=True):
                return eng.matmul(o, w, v, start=start, stop=stop, skip_group_check=True)

            eng.sem_inc(s_free, RING)
            for count in (s_ep, s_ep_out, c_used):
                eng.sem_inc(count, 1)
            eng.wait_ge(s_const, 5)

            def chunk(c, K, flag):
                cs = slice(c * P, (c + 1) * P)
                A, B = EA[c % 2], EB[c % 2]
                gate3 = A[:, 0:3 * P].rearrange("p (g n) -> p g n", g=3)[:, :, 0:H]
                if c >= 2:
                    eng.wait_ge(s_ep_out, 2 * (CH * K + c - 1) + 1)
                mm(A[:, :], ones[0:H, :], bias_split[:, :], start=True)
                mm(A[:, :], xt_split[:, cs], w_h_hi[:, :])
                mm(A[:, :], xt_split[:, cs], w_h_lo[:, :])
                mm(gate3, plus_sb[:, cs], w_plus[:, :].rearrange("p (g f) -> p g f", g=3))
                with eng.If(flag > 0):
                    mm(gate3, minus_sb[:, cs], w_minus[:, :].rearrange("p (g f) -> p g f", g=3))
                    mm(B[:, 196:196 + 3 * H], nvalue_sb[:, cs], w_value[:, :], start=True)
                    mm(B[:, 195:196], ncount_sb[:, cs], ident[0:1, 0:1], start=True)
                    mm(B[:, 192:194], minus_sb[:, cs], a_minus[:, :], start=True)
                    mm(B[:, 192:194], plus_sb[:, cs], a_plus[:, :])
                with eng.Else():
                    mm(B[:, 192:194], plus_sb[:, cs], a_plus[:, :], start=True)
                mm(B[:, 194:195], count_sb[:, cs], ident[0:1, 0:1], start=True)
                mm(B[:, 0:3 * H], value_sb[:, cs], w_value[:, :], start=True).then_inc(s_ep, 1)

            def last_steps(q, K, flag):
                if q == PE_ABOVE:
                    eng.wait_ge(s_above, K + 1)
                    eng.wait_ge(s_ep_out, 2 * CH * K + 1)
                    eng.transpose(EB[0][0:1, 0:P], above_max[:, :], ident[:, :]).then_inc(s_above_t, 1)
                if q == PE_FLAG:
                    flag = load_flag(eng, K)
                    with eng.If(flag > 0):
                        for k in range(TILES):
                            eng.wait_ge(c_dve, 3 * (TILES * K + k + 1))
                            mm(EA[0][:, :], h_split[:, k, :], c_mask[:, :], start=(k == 0))
                            mm(EA[1][:, :], ones[:, :], c_mask[:, :], start=(k == 0))
                            mm(EB[1][:, :], h_split[:, k, :], c_hi[:, :], start=(k == 0))
                            mm(EB[1][:, :], h_split[:, k, :], c_lo[:, :]).then_inc(c_used, 1)
                    with eng.Else():
                        eng.sem_inc(c_used, TILES)
                if q == PE_CHUNKS:
                    eng.wait_ge(s_evac, 4 * (K + 1))
                    eng.wait_ge(c_out, 3 * (K + 1))
                    eng.wait_ge(s_xt, K + 1)
                    chunk(0, K, flag)
                    chunk(1, K, flag)
                if q == PE_CHUNKS + 1:
                    chunk(2, K, flag)
                    chunk(3, K, flag)
                return flag

            def one_block(I, K):
                flag = None
                for q in range(UNITS):
                    g = UNITS * I + q
                    u = unit_at(q)
                    J, s = u // UPB, q % RING
                    parts = [(UT * u + t, slice(t * BI, (t + 1) * BI), q == 0 and t == 0) for t in range(UT)]
                    if K is None and q == 0:
                        eng.wait_ge(s_h_first, 2)
                    if K is None and q == UPB:
                        eng.wait_ge(s_h_rest, 2)
                    eng.wait_ge(s_mask, g + 1)
                    if q == 0 and K is not None:
                        eng.wait_ge(s_evac, 4 * K + 1)
                    for j, v, first in parts:
                        mm(PLUS[:, :], h_split[:, j, :], mask[:, s, v], start=first)
                    if q == 0 and K is not None:
                        eng.wait_ge(s_evac, 4 * K + 2)
                    for j, v, first in parts:
                        mm(COUNT[:, :], ones[:, :], mask[:, s, v], start=first)
                    eng.wait_ge(s_lo, g + 1)
                    if q == 0:
                        if K is not None:
                            eng.wait_ge(s_evac, 4 * K + 4)
                        mm(AX1[:, :], zero_w[:, :], hi[:, s, 0:BI], start=True)
                    if K is not None and J + lag(J) < BLOCKS - 1:
                        with eng.If(I > J + lag(J)):
                            eng.wait_ge(s_x1, 2 * (J + 1))
                            for j, v, first in parts:
                                mm(AX1[:, :], x1_split[:, j, :], hi[:, s, v])
                                mm(AX1[:, :], x1_split[:, j, :], lo[:, s, v])
                    for j, v, first in parts:
                        mm(VALUE[:, :], h_split[:, j, :], hi[:, s, v], start=first)
                        last = mm(VALUE[:, :], h_split[:, j, :], lo[:, s, v])
                    last.then_inc(s_free, 1)
                    if K is not None:
                        flag = last_steps(q, K, flag)
                    elif q == 10:
                        eng.wait_ge(s_setup_d, 7 * 16)
                        mm(EA[0][:, 0:3 * H + 2], w_gat_t[:, :], gat[:, :], start=True).then_inc(s_w, 1)

            one_block(0, None)
            eng.wait_ge(s_wsplit, 8)
            with eng.Fori(1, BLOCKS) as I:
                one_block(I, I - 1)

            eng.wait_ge(s_evac, 4 * BLOCKS)

            def finish(F):
                eng.wait_ge(s_ax_sb, F + 1)
                if F >= 2:
                    eng.wait_ge(s_fin_rd, F - 1)
                for c in range(CH):
                    o = bank[2 + F % 2][:, c * H:(c + 1) * H]
                    mm(o, ax_part[:, F, c * P:(c + 1) * P], pair_ident[:, :], start=True)
                    last = mm(o, ax_sb[:, c * P:(c + 1) * P], pair_ident[:, :])
                last.then_inc(s_fin, 1)

            flag = None
            for n, (I, J, h) in enumerate(UNITS2):
                s = n % RING
                first = n == 0 or UNITS2[n - 1][0] != I
                if first and I >= 2:
                    eng.wait_ge(s_ax_sb, I - 1)
                if h == 0:
                    eng.wait_ge(s_x1, 2 * (J + 1))
                eng.wait_ge(s_lo2, n + 1)
                for t in range(UT):
                    j = UT * (UPB * J + h) + t
                    v = slice(t * BI, (t + 1) * BI)
                    mm(bank[I % 2][:, :], x1_split[:, j, :], hi[:, s, v], start=first and t == 0)
                    last = mm(bank[I % 2][:, :], x1_split[:, j, :], lo[:, s, v])
                last.then_inc(s_free, 1)
                flag = last_steps(n, BLOCKS - 1, flag)
                for F in ended(n, 2):
                    finish(F)


def kernel(x, adj, L0_gnn_W_gat, L0_gnn_a_gat, L0_gnn_w_ih_e, L0_gnn_w_hh_e, L0_gnn_b_ih_e,
           L0_gnn_b_hh_e, L0_gnn_w_ih_n, L0_gnn_w_hh_n, L0_gnn_b_ih_n, L0_gnn_b_hh_n, L1_gnn_t):
    import numpy as np
    import concourse.bacc as bacc
    from concourse.bass_utils import run_bass_kernel_spmd as run

    N, H = x.shape
    P, BI, UT = 128, 512, 2
    B = N // BI
    x, adj = np.asarray(x), np.asarray(adj)

    def gates(e, n, parts):
        e3, n3 = (np.asarray(a).T.reshape(-1, 3, H) for a in (e, n))
        full = np.zeros((e3.shape[0], 4, 2, H), np.float32)
        for third, part in enumerate(parts):
            full[:, part, 0] = e3[:, third]
            full[:, part, 1] = n3[:, third]
        return full.reshape(-1, 8 * H)

    w_ih_e = np.asarray(L0_gnn_w_ih_e).T
    w_h = gates(L0_gnn_w_hh_e, L0_gnn_w_hh_n, (0, 1, 3))
    b_hh = gates(np.asarray(L0_gnn_b_hh_e)[:, None], np.asarray(L0_gnn_b_hh_n)[:, None], (0, 1, 3))
    b_ih = gates(np.asarray(L0_gnn_b_ih_e)[:, None], np.asarray(L0_gnn_b_ih_n)[:, None], (0, 1, 2))
    bias = np.zeros((H, 8 * H), np.float32)
    bias[0:2] = bias[32:34] = np.concatenate([b_hh, b_ih])
    a = np.asarray(L0_gnn_a_gat).reshape(2, H).T
    w_gat_t = np.asarray(L0_gnn_W_gat).T
    xt = np.ascontiguousarray(x.T).reshape(H, B, BI).transpose(1, 0, 2)
    arrays = {
        "adj_t": adj.reshape(B, BI, N // (UT * P), UT, P).transpose(0, 2, 4, 3, 1),
        "x_rows_d": x.reshape(N // P, P, H).transpose(1, 0, 2),
        "x_t_d": np.concatenate([xt, xt], axis=1),
        "diag_d": np.diagonal(adj).reshape(N // P, P).T,
        "gat_d": np.concatenate([np.asarray(L0_gnn_w_ih_n).T, a], axis=1),
        "w_gat_t_d": np.concatenate([w_gat_t, w_gat_t], axis=1),
        "w_plus_d": np.concatenate([w_ih_e[:H], w_ih_e[:H]]),
        "w_minus_d": np.concatenate([w_ih_e[H:], w_ih_e[H:]]),
        "w_h_d": np.concatenate([w_h, w_h]),
        "bias_d": bias,
    }
    arrays = {name: np.ascontiguousarray(v) for name, v in arrays.items()}
    nc = bacc.Bacc("TRN2", target_bir_lowering=False, num_devices=1)
    args = [nc.dram_tensor(name, v.shape, mybir.dt.from_np(v.dtype), kind="ExternalInput").ap()
            for name, v in arrays.items()]
    out = nc.dram_tensor("out", (N, H), mybir.dt.float32, kind="ExternalOutput").ap()
    gnn_ode_kernel(nc, *args, out)
    return run(nc, [arrays], core_ids=[0]).results[0]["out"]
```

```python
import concourse.bass as bass
from concourse import mybir
from contextlib import ExitStack

NEG_INF = -9.0e15
ALPHA = 0.2
EPS = 1e-5
AWAY = 1.0 + 2.0 ** -12


def gnn_ode_kernel(nc: bass.Bass, adj_t, x_rows_d, x_t_d, diag_d, gat_d, w_gat_t_d, w_plus_d,
                   w_minus_d, w_h_d, bias_d, out):
    fp32, f32r, i32 = mybir.dt.float32, mybir.dt.float32r, mybir.dt.int32
    bf16 = mybir.dt.bfloat16
    ALU, ACT, AX = mybir.AluOpType, mybir.ActivationFunctionType, mybir.AxisListType

    BLOCKS, UNITS, P, UT, BI = adj_t.shape
    N = BLOCKS * BI
    TILES = N // P
    CH = BI // P
    UPB = UNITS // BLOCKS
    H = 64
    UW = UT * BI
    RAW = 8
    RING = 6

    ctx = ExitStack()
    with ctx:
        def sb(name, shape, dt=fp32):
            return ctx.enter_context(nc.sbuf_tensor(name, shape, dt))

        def sem(name):
            return ctx.enter_context(nc.semaphore(name))

        raw = sb("raw", [P, RAW, UW])
        mask = sb("mask", [P, RING, UW], f32r)
        hi = sb("hi", [P, RING, UW], f32r)
        lo = sb("lo", [P, RING, UW], f32r)
        h_split = sb("h_split", [P, TILES, 2 * H], f32r)
        x1_split = sb("x1_split", [P, TILES, 2 * H], f32r)
        x_rows = sb("x_rows", [P, TILES, H])
        x1_rows = x_rows
        ax_part = sb("ax_part", [P, BLOCKS - 2, BI])
        diag = sb("diag", [P, TILES])
        xt_raw = sb("xt_raw", [P, BI])
        xt_split = sb("xt_split", [P, BI], f32r)
        ones = sb("ones", [P, P], f32r)
        ones16 = sb("ones16", [P, P // 4], bf16)
        quarters = sb("quarters", [P, 1])
        ident = sb("ident", [P, P])
        pair_ident = sb("pair_ident", [P, H])
        zero_w = sb("zero_w", [P, P], f32r)
        gat = sb("gat", [H, 3 * H + 2])
        w_gat_t = sb("w_gat_t", [H, 2 * H])
        w_plus = sb("w_plus", [P, 3 * H])
        w_minus = sb("w_minus", [P, 3 * H])
        w_value = sb("w_value", [P, 3 * H])
        a_plus = sb("a_plus", [P, 2])
        a_minus = sb("a_minus", [P, 2])
        minus_sb = sb("minus_sb", [P, BI])
        w_h_raw = minus_sb[:, 0:3 * P]
        w_h_hi = sb("w_h_hi", [P, 3 * P], f32r)
        w_h_lo = sb("w_h_lo", [P, 3 * P], f32r)
        bias_raw = sb("bias_raw", [H, 4 * P])
        bias_split = sb("bias_split", [H, 4 * P], f32r)
        plus_sb = sb("plus_sb", [P, BI])
        value_sb = sb("value_sb", [P, BI])
        count_sb = sb("count_sb", [P, BI])
        ncount_sb = bias_raw[0:1, :]
        nvalue_sb = sb("nvalue_sb", [P, BI])
        gates = sb("gates", [P, CH, 4, P])
        vals = sb("vals", [P, CH, 388])
        vals_flat = vals[:, :, :].rearrange("p c n -> p (c n)")
        above = sb("above", [P, UNITS])
        above_max = sb("above_max", [P, 1])
        above_all = sb("above_all", [1, 1])
        has_minus = sb("has_minus", [1, BLOCKS], i32)
        leaky = sb("leaky", [P, CH, 2])
        absent = sb("absent", [P, CH, 2])
        top = sb("top", [P, CH, 1])
        expo = sb("expo", [P, CH, 3])
        cnt = sb("cnt", [P, CH, 3])
        norm = sb("norm", [P, CH, 1])
        att = sb("att", [P, CH, 3])
        y = sb("y", [P, CH, H])
        sq = sb("sq", [P, CH, H])
        row_sum = sb("row_sum", [P, CH, 1])
        stats = sb("stats", [P, CH, 6])
        moments = sb("moments", [P, CH, 2])
        mix = sb("mix", [P, CH, 2, H])
        ode = sb("ode", [P, CH, H])
        var = sb("var", [P, CH, 1])
        rstd = sb("rstd", [P, CH, 1])
        neg_half = sb("neg_half", [P, CH, 1])
        ax_sb = value_sb
        res = vals_flat[:, 0:2 * CH * H].rearrange("p (s c f) -> p s c f", s=2, c=CH)
        c_raw = gates[:, 0:1].rearrange("p a b c -> p (a b c)")
        c_mask = x1_split[:, TILES - CH:, :].rearrange("p c n -> p (c n)")
        c_hi = sb("c_hi", [P, BI], f32r)
        c_lo = sb("c_lo", [P, BI], f32r)

        bank = [ctx.enter_context(nc.psum_tensor(f"bank{n}", [P, BI], fp32)) for n in range(8)]
        PLUS, COUNT, VALUE, AX1 = bank[0:4]
        EA, EB = bank[4:6], bank[6:8]

        s_raw = [sem(f"s_raw{n}") for n in range(RAW)]
        s_x_first = sem("s_x_first")
        s_x_rest = sem("s_x_rest")
        s_h_first = sem("s_h_first")
        s_h_rest = sem("s_h_rest")
        s_setup_d = sem("s_setup_d")
        s_const = sem("s_const")
        s_w = sem("s_w")
        s_wsplit = sem("s_wsplit")
        s_diag = sem("s_diag")
        s_tile = sem("s_tile")
        s_mask = sem("s_mask")
        s_hi = sem("s_hi")
        s_lo = sem("s_lo")
        s_free = sem("s_free")
        s_evac = sem("s_evac")
        s_above = sem("s_above")
        s_above_t = sem("s_above_t")
        s_flag = sem("s_flag")
        s_seen = sem("s_seen")
        s_xt_d = sem("s_xt_d")
        s_xt = sem("s_xt")
        s_ep = sem("s_ep")
        s_ep_out = sem("s_ep_out")
        s_expo = sem("s_expo")
        s_exp = sem("s_exp")
        s_gin = sem("s_gin")
        s_act = sem("s_act")
        s_nin = sem("s_nin")
        s_y = sem("s_y")
        s_sum = sem("s_sum")
        s_ode = sem("s_ode")
        s_x1r = sem("s_x1r")
        s_var = sem("s_var")
        s_rstd = sem("s_rstd")
        s_x1 = sem("s_x1")
        s_xt_hi = sem("s_xt_hi")
        s_dve = sem("s_dve")
        s_dve2 = sem("s_dve2")
        s_pool = sem("s_pool")
        c_dma = sem("c_dma")
        c_diag = sem("c_diag")
        c_tile = sem("c_tile")
        c_dve = sem("c_dve")
        c_used = sem("c_used")
        c_out = sem("c_out")
        s_hi2 = sem("s_hi2")
        s_lo2 = sem("s_lo2")
        s_ax_sb = sem("s_ax_sb")
        s_fin = sem("s_fin")
        s_fin_rd = sem("s_fin_rd")
        s_res = sem("s_res")
        s_out = [sem(f"s_out{n}") for n in range(2)]

        def unit_at(q):
            return UPB * (BLOCKS - 1 - q // UPB) + q % UPB

        ORDER2 = [0, 1] + list(range(BLOCKS - 1, 1, -1))
        UNITS2 = [(k, J, h) for k in range(BLOCKS) for J in range(BLOCKS)
                  if ORDER2[k] <= J + 1 for h in range(UPB)]
        UNITS2.sort(key=lambda u: (u[0] // 2, u[0] < 2 and u[1] == BLOCKS - 1, u[0]))
        FIRST2 = [min(n for n, u in enumerate(UNITS2) if u[0] == k) for k in range(BLOCKS)]
        LAST2 = [max(n for n, u in enumerate(UNITS2) if u[0] == k) for k in range(BLOCKS)]
        END2 = len(UNITS2) - 1
        LOADS1 = BLOCKS * UNITS
        FIRST = TILES - CH

        def used_before(q):
            if q >= RING:
                return q - RING
            return max(p for p in range(UNITS) if p % RING == q) - UNITS

        def ended(n, *behind):
            return [(k, step) for k in range(BLOCKS) for step, b in enumerate(behind)
                    if LAST2[k] + b == n or (n == END2 and LAST2[k] + b > n)]

        PE_ABOVE, PE_FLAG, PE_CHUNKS = 1, 3, (3, 3, 4, 4)
        DVE_FLAG, DVE_BRANCH, DVE_EXPO, DVE_ATT, DVE_N, DVE_NORM, DVE_X1 = 3, 4, 9, 9, 10, 16, 18
        ACT_SUMS, ACT_FLAG, ACT_CHUNKS, ACT_EXP, ACT_RZ, ACT_N = 2, 6, (8, 8, 9, 9), 10, 11, 12
        POOL_FIX, POOL_Y, POOL_POWER = 7, 15, 18
        POOL_XT_LOAD, ACT_XT, POOL_XT = 7, 9, 12
        STRETCH = 1.2
        PE_END, ACT_END, DVE_END = 3, 5, (7, 9)

        def stretched(n):
            return [q for q in range(2 * UNITS) if int(STRETCH * q) == n]

        block = ctx.enter_context(nc.Block())

        def seen(eng):
            eng.sem_inc(s_seen, 1)

        def bc(ap, n):
            return ap.to_broadcast([P, CH, n])

        def load_flag(eng, K):
            eng.wait_ge(s_flag, K + 1)
            seen(eng)
            return eng.value_load(has_minus[0:1, bass.ds(K, 1)])

        @block.sync
        def _(eng):
            def load(slot, src):
                eng.dma_start(raw[:, slot, :], src.rearrange("p t i -> p (t i)")).then_inc(s_raw[slot], 16)

            eng.dma_start(x_rows[:, FIRST:, :], x_rows_d[:, FIRST:, :]).then_inc(s_x_first, 16)
            for q in range(UPB):
                load(q, adj_t[0, unit_at(q), :, :, :])
            eng.dma_start(x_rows[:, :FIRST, :], x_rows_d[:, :FIRST, :]).then_inc(s_x_rest, 16)
            for q in range(UPB, RAW):
                load(q, adj_t[0, unit_at(q), :, :, :])
            eng.dma_start(gat[:, :], gat_d).then_inc(s_setup_d, 16)
            eng.dma_start(w_gat_t[:, :], w_gat_t_d).then_inc(s_setup_d, 16)
            eng.dma_start(w_plus[:, :], w_plus_d).then_inc(s_setup_d, 16)
            eng.dma_start(w_minus[:, :], w_minus_d).then_inc(s_setup_d, 16)
            eng.dma_start(w_h_raw[:, :], w_h_d).then_inc(s_setup_d, 16)
            eng.dma_start(bias_raw[:, :], bias_d).then_inc(s_setup_d, 16)
            eng.dma_start(diag[:, :], diag_d).then_inc(s_setup_d, 16)
            with eng.Fori(0, BLOCKS - 1) as I:
                for q in range(UNITS):
                    eng.wait_ge(s_lo, UNITS * I + q + 1)
                    seen(eng)
                    n = q + RAW
                    if n < UNITS:
                        load(n % RAW, adj_t[I, unit_at(n), :, :, :])
                    else:
                        load(n % RAW, adj_t[I + 1, unit_at(n - UNITS), :, :, :])
            for q in range(UNITS - RAW):
                eng.wait_ge(s_lo, UNITS * (BLOCKS - 1) + q + 1)
                load(q % RAW, adj_t[BLOCKS - 1, unit_at(q + RAW), :, :, :])
            for n, (k, J, h) in enumerate(UNITS2):
                if n < RAW:
                    eng.wait_ge(s_lo, LOADS1 - RAW + n + 1)
                else:
                    eng.wait_ge(s_lo2, n - RAW + 1)
                load(n % RAW, adj_t[ORDER2[k], UPB * J + h, :, :, :])

        @block.gpsimd
        def _(eng):
            eng.memset(ident[:, :], 0.0).then_inc(s_pool, 1)
            eng.memset(pair_ident[:, :], 0.0).then_inc(s_pool, 1)
            eng.memset(neg_half[:, :, :], -0.5).then_inc(s_const, 1)
            eng.wait_ge(s_pool, 2)
            eng.affine_select(out=ident[:, :], in_=ident[:, :], compare_op=ALU.not_equal, fill=1.0,
                              base=0, pattern=[[-1, P]], channel_multiplier=1).then_inc(s_const, 1)
            eng.affine_select(out=pair_ident[:, :], in_=pair_ident[:, :], compare_op=ALU.not_equal,
                              fill=1.0, base=0, pattern=[[-1, H]], channel_multiplier=1).then_inc(s_pool, 1)
            eng.wait_ge(s_pool, 3)
            eng.affine_select(out=pair_ident[:, :], in_=pair_ident[:, :], compare_op=ALU.not_equal,
                              fill=1.0, base=-H, pattern=[[-1, H]], channel_multiplier=1).then_inc(s_const, 1)
            POOL0, POOL_PER = 3, 6
            links = [0]

            def link(ins, K):
                links[0] += 1
                ins.then_inc(s_pool, 1)
                eng.wait_ge(s_pool, POOL_PER * K + POOL0 + links[0])

            def zero_diagonal(ap, q, s):
                part = ap[:, q * P:(q + 1) * P]
                eng.affine_select(out=part, in_=part, compare_op=ALU.not_equal, fill=0.0, base=0,
                                  pattern=[[-1, P]], channel_multiplier=1).then_inc(s, 1)

            def power():
                eng.tensor_tensor(rstd[:, :, :], var[:, :, :], neg_half[:, :, :], ALU.pow).then_inc(s_rstd, 1)

            def last_steps(q, K):
                if q == POOL_FIX:
                    flag = load_flag(eng, K)
                    with eng.If(flag > 0):
                        for J in range(BLOCKS):
                            for t in range(CH):
                                eng.wait_ge(c_dma, 16 * (TILES * K + CH * J + t + 1))
                                seen(eng)
                                with eng.If(K == J):
                                    zero_diagonal(c_raw, t, c_diag)
                                    eng.wait_ge(c_diag, CH * K + t + 1)
                                eng.sem_inc(c_tile, 1)
                    with eng.Else():
                        eng.sem_inc(c_tile, TILES)
                        eng.sem_inc(c_diag, CH)
                if q == POOL_Y:
                    links[0] = 0
                    eng.wait_ge(s_act, 3 * K + 3)
                    seen(eng)
                    xb = x_rows[:, bass.ds(CH * K, CH), :]
                    n_out = gates[:, :, 0, :].rearrange("p c (e f) -> p c e f", e=2)
                    z = gates[:, :, 2, :].rearrange("p c (e f) -> p c e f", e=2)
                    link(eng.tensor_tensor(mix[:, :, 0, :], xb, n_out[:, :, 0, :], ALU.subtract), K)
                    seen(eng)
                    link(eng.tensor_tensor(mix[:, :, 1, :], xb, n_out[:, :, 1, :], ALU.subtract), K)
                    link(eng.tensor_tensor(mix[:, :, :, :], mix[:, :, :, :], z, ALU.mult), K)
                    link(eng.tensor_tensor(mix[:, :, :, :], mix[:, :, :, :], n_out, ALU.add), K)
                    link(eng.tensor_tensor(y[:, :, :], mix[:, :, 0, :], mix[:, :, 1, :], ALU.add), K)
                    seen(eng)
                    link(eng.tensor_tensor(y[:, :, :], y[:, :, :],
                                           bc(diag[:, bass.ds(CH * K, CH)].rearrange("p (c o) -> p c o", o=1), H),
                                           ALU.mult), K)
                    seen(eng)
                    eng.tensor_tensor(y[:, :, :], y[:, :, :], xb, ALU.add).then_inc(s_y, 1)
                    assert links[0] == POOL_PER, links[0]
                if q == POOL_POWER:
                    eng.wait_ge(s_var, K + 1)
                    power()
                    x1b = x1_rows[:, bass.ds(CH * K, CH), :]
                    seen(eng)
                    eng.tensor_tensor(x1b, y[:, :, :], bc(moments[:, :, 0:1], H), ALU.subtract).then_inc(s_x1r, 1)
                    eng.wait_ge(s_x1r, 2 * K + 1)
                    eng.wait_ge(s_rstd, K + 1)
                    seen(eng)
                    eng.tensor_tensor(x1b, x1b, bc(rstd[:, :, :], H), ALU.mult).then_inc(s_x1r, 1)

            def one_block(I, K):
                for q in range(UNITS):
                    J, h = unit_at(q) // UPB, unit_at(q) % UPB
                    eng.wait_ge(s_raw[q % RAW], 16 * ((UNITS // RAW) * I + q // RAW + 1))
                    seen(eng)

                    def own_columns():
                        for t in range(UT):
                            zero_diagonal(raw[:, q % RAW, t * BI:(t + 1) * BI], UT * h + t, s_diag)
                        eng.wait_ge(s_diag, CH * I + UT * (h + 1))

                    if isinstance(I, int):
                        if J == I:
                            own_columns()
                    else:
                        with eng.If(I == J):
                            own_columns()
                    eng.sem_inc(s_tile, 1)
                    if q == POOL_XT_LOAD:
                        eng.dma_start(xt_raw[:, :], x_t_d[I]).then_inc(s_xt_d, 16)
                    if q == POOL_XT:
                        if not isinstance(I, int):
                            eng.wait_ge(s_x1r, 2 * (I - 1))
                        eng.wait_ge(s_xt_hi, I + 1)
                        eng.tensor_tensor(xt_split[H:P, :], xt_raw[H:P, :], xt_split[H:P, :].bitcast(fp32),
                                          ALU.subtract).then_inc(s_xt, 1)
                        eng.wait_ge(s_xt, I + 1)
                    if K is not None:
                        if not isinstance(I, int):
                            last_steps(q + UNITS, I - 2)
                        last_steps(q, K)
            one_block(0, None)
            eng.wait_ge(s_setup_d, 7 * 16)
            one_block(1, 0)
            with eng.Fori(2, BLOCKS) as I:
                one_block(I, I - 1)
            for q in range(2 * UNITS):
                last_steps(q + UNITS, BLOCKS - 2)
                last_steps(q, BLOCKS - 1)
            for n in range(BLOCKS):
                I = ORDER2[n]
                x1b = x1_rows[:, CH * I:CH * (I + 1), :]
                if n == 0:
                    eng.wait_ge(s_x1r, 2 * BLOCKS)
                eng.tensor_scalar(ode[:, :, :], x1b, -0.1, 1.0, ALU.mult, ALU.add).then_inc(s_ode, 1)
                eng.wait_ge(s_ode, 2 * n + 1)
                eng.tensor_tensor(ode[:, :, :], ode[:, :, :], x1b, ALU.add).then_inc(s_ode, 1)
                eng.wait_ge(s_ode, 2 * n + 2)
                eng.wait_ge(s_sum, n + 1)
                eng.tensor_tensor(y[:, :, :], ode[:, :, :], bc(row_sum[:, :, :], H),
                                  ALU.subtract).then_inc(s_y, 1)
                eng.wait_ge(s_var, BLOCKS + n + 1)
                power()
                if n >= 2:
                    eng.wait_ge(s_out[n % 2], 16 * (n // 2))
                rows = res[:, n % 2, :, :]
                eng.tensor_tensor(rows, y[:, :, :], bc(moments[:, :, 0:1], H), ALU.subtract).then_inc(s_res, 1)
                eng.wait_ge(s_rstd, BLOCKS + n + 1)
                eng.wait_ge(s_res, 2 * n + 1)
                eng.tensor_tensor(rows, rows, bc(rstd[:, :, :], H), ALU.mult).then_inc(s_res, 1)
                eng.wait_ge(s_res, 2 * n + 2)
                eng.dma_start(out[I * BI:(I + 1) * BI, :].rearrange("(c p) f -> p c f", p=P),
                              rows).then_inc(s_out[n % 2], 16)
            for done in s_out:
                eng.wait_ge(done, 16 * BLOCKS // 2)

        @block.scalar
        def _(eng):
            eng.wait_ge(s_x_first, 16)
            eng.activation(h_split[:, FIRST:, 0:H], x_rows[:, FIRST:, :], ACT.Copy).then_inc(s_h_first, 1)

            def first_steps(q):
                if q == 1:
                    eng.wait_ge(s_x_rest, 16)
                    eng.activation(h_split[:, :FIRST, 0:H], x_rows[:, :FIRST, :], ACT.Copy).then_inc(s_h_rest, 1)
                if q == 8:
                    eng.wait_ge(s_setup_d, 7 * 16)
                    eng.activation(w_h_hi[:, :], w_h_raw[:, :], ACT.Copy).then_inc(s_wsplit, 1)

            def copy_chunk(c, K, flag):
                eng.wait_ge(s_ep, CH * K + c + 2)
                eng.activation(gates[:, c, :, :].rearrange("p g n -> p (g n)"), EA[c % 2][:, :],
                               ACT.Copy).then_inc(s_ep_out, 1)
                with eng.If(flag > 0):
                    eng.activation(vals[:, c, :], EB[c % 2][:, 0:388], ACT.Copy).then_inc(s_ep_out, 1)
                with eng.Else():
                    eng.activation(vals[:, c, 0:195], EB[c % 2][:, 0:195], ACT.Copy).then_inc(s_ep_out, 1)

            def last_steps(q, K, flag):
                if q == ACT_SUMS:
                    eng.wait_ge(s_free, UNITS * (K + 1) - 1)
                    eng.activation(plus_sb[:, :], PLUS[:, :], ACT.Copy).then_inc(s_evac, 1)
                    eng.activation(count_sb[:, :], COUNT[:, :], ACT.Copy).then_inc(s_evac, 1)
                    eng.wait_ge(s_free, UNITS * (K + 1))
                    eng.activation(value_sb[:, :], VALUE[:, :], ACT.Copy).then_inc(s_evac, 1)
                    eng.activation(ax_part[:, bass.ds((K + BLOCKS - 4) % (BLOCKS - 2), 1), :].rearrange("p a i -> p (a i)"), AX1[:, :],
                                   ACT.Copy).then_inc(s_evac, 1)
                if q == ACT_FLAG:
                    flag = load_flag(eng, K)
                    with eng.If(flag > 0):
                        with eng.Fori(0, UNITS) as u:
                            for t in range(UT):
                                eng.wait_ge(c_used, TILES * K + UT * u + t + 1)
                                eng.dma_start(c_raw, adj_t[K, u, :, t, :]).then_inc(c_dma, 16)
                    with eng.Else():
                        eng.sem_inc(c_dma, 16 * TILES)
                for c in range(CH):
                    if q == ACT_CHUNKS[c]:
                        copy_chunk(c, K, flag)
                if q == ACT_EXP:
                    eng.wait_ge(s_expo, 2 * K + 2)
                    eng.activation(expo[:, :, :], expo[:, :, :], ACT.Exp).then_inc(s_exp, 1)
                if q == ACT_RZ:
                    eng.wait_ge(s_gin, 2 * CH * (K + 1))
                    eng.activation(gates[:, :, 1:3, :], gates[:, :, 1:3, :], ACT.Tanh,
                                   scale=0.5).then_inc(s_act, 1)
                    eng.wait_ge(s_act, 3 * K + 1)
                    eng.activation(gates[:, :, 2, :], gates[:, :, 2, :], ACT.Copy, bias=0.5,
                                   scale=0.5).then_inc(s_act, 1)
                if q == ACT_N:
                    eng.wait_ge(s_nin, K + 1)
                    eng.activation(gates[:, :, 0, :], gates[:, :, 0, :], ACT.Tanh).then_inc(s_act, 1)
                return flag

            def one_block(I, K):
                flag = None
                for q in range(UNITS):
                    g = UNITS * I + q
                    eng.wait_ge(s_tile, g + 1)
                    if K is not None or q >= RING:
                        eng.wait_ge(s_free, UNITS * I + used_before(q) + 1)
                    eng.activation(hi[:, q % RING, :], raw[:, q % RAW, :], ACT.Copy,
                                   scale=AWAY).then_inc(s_hi, 1)
                    if K is not None:
                        flag = last_steps(q, K, flag)
                    else:
                        first_steps(q)
                    if q == ACT_XT:
                        eng.wait_ge(s_xt_d, 16 * (I + 1))
                        eng.wait_ge(s_ep, CH * I + 1)
                        eng.activation(xt_split[:, :], xt_raw[:, :], ACT.Copy).then_inc(s_xt_hi, 1)

            one_block(0, None)
            with eng.Fori(1, BLOCKS) as I:
                one_block(I, I - 1)
            flag = None
            for n, (k, J, h) in enumerate(UNITS2):
                eng.wait_ge(s_raw[n % RAW], 16 * (LOADS1 // RAW + n // RAW + 1))
                eng.wait_ge(s_free, LOADS1 + used_before(n) + 1)
                eng.activation(hi[:, n % RING, :], raw[:, n % RAW, :], ACT.Copy).then_inc(s_hi2, 1)
                for q in stretched(n):
                    flag = last_steps(q, BLOCKS - 1, flag)
                for k, _ in ended(n, ACT_END):
                    eng.wait_ge(s_free, LOADS1 + LAST2[k] + 1)
                    if k:
                        eng.wait_ge(s_fin, k)
                    eng.activation(ax_sb[:, :], bank[k % 2][:, :], ACT.Copy).then_inc(s_ax_sb, 1)

        @block.vector
        def _(eng):
            eng.memset(mask[:, 0, 0:P].bitcast(fp32), 1.0).then_inc(s_dve, 1)
            eng.memset(zero_w[:, :].bitcast(fp32), 0.0).then_inc(s_const, 1)
            eng.memset(ones16[:, :], 1.0).then_inc(s_const, 1)
            eng.memset(quarters[:, :], 4.0 / P).then_inc(s_const, 1)
            eng.memset(bias_split[:, :].bitcast(fp32), 0.0).then_inc(s_dve, 1)
            eng.wait_ge(s_dve, 2)
            eng.tensor_copy(ones[:, :], mask[:, 0, 0:P].bitcast(fp32)).then_inc(s_const, 1)
            eng.wait_ge(s_const, 7)
            eng.wait_ge(s_h_first, 1)
            eng.tensor_tensor(h_split[:, FIRST:, H:2 * H], x_rows[:, FIRST:, :],
                              h_split[:, FIRST:, 0:H].bitcast(fp32), ALU.subtract).then_inc(s_h_first, 1)

            def first_steps(q):
                if q == 1:
                    eng.wait_ge(s_h_rest, 1)
                    eng.tensor_tensor(h_split[:, :FIRST, H:2 * H], x_rows[:, :FIRST, :],
                                      h_split[:, :FIRST, 0:H].bitcast(fp32), ALU.subtract).then_inc(s_h_rest, 1)
                if q == 9:
                    eng.wait_ge(s_wsplit, 1)
                    eng.tensor_tensor(w_h_lo[:, :], w_h_raw[:, :], w_h_hi[:, :].bitcast(fp32),
                                      ALU.subtract).then_inc(s_wsplit, 1)
                    eng.tensor_copy(bias_split[0:2, :], bias_raw[0:2, :]).then_inc(s_wsplit, 1)
                    eng.tensor_copy(bias_split[32:34, :], bias_raw[32:34, :]).then_inc(s_dve, 1)
                    eng.wait_ge(s_dve, 3)
                    eng.tensor_tensor(bias_split[32:34, :], bias_raw[32:34, :],
                                      bias_split[32:34, :].bitcast(fp32), ALU.subtract).then_inc(s_wsplit, 1)
                if q == 14:
                    eng.wait_ge(s_w, 1)
                    eng.tensor_copy(w_value[:, :], EA[0][:, 0:3 * H]).then_inc(s_wsplit, 1)
                    eng.tensor_copy(a_plus[:, :], EA[0][:, 3 * H:3 * H + 2]).then_inc(s_wsplit, 1)
                    eng.tensor_copy(a_minus[:, 0:1], EA[0][:, 3 * H + 1:3 * H + 2]).then_inc(s_wsplit, 1)
                    eng.tensor_copy(a_minus[:, 1:2], EA[0][:, 3 * H:3 * H + 1]).then_inc(s_wsplit, 1)

            BASE = 3
            PER_BLOCK = 23
            links = [0]
            links2 = [0]

            def mark(ins):
                links[0] += 1
                ins.then_inc(s_dve, 1)

            def join(K):
                eng.wait_ge(s_dve, PER_BLOCK * K + BASE + links[0])

            def link(ins, K):
                mark(ins)
                join(K)

            def mark2(ins):
                links2[0] += 1
                ins.then_inc(s_dve2, 1)

            def join2(K=None):
                eng.wait_ge(s_dve2, links2[0])

            def moments_of_y(mark, join, K):
                for c in range(CH):
                    mark(eng.bn_stats(stats[:, c, :], y[:, c, :]))
                join(K)
                seen(eng)
                for c in range(CH):
                    mark(eng.bn_aggr(moments[:, c, :], stats[:, c, :]))
                join(K)
                eng.tensor_scalar(var[:, :, :], moments[:, :, 1:2], EPS, None, ALU.add).then_inc(s_var, 1)

            def correct(K):
                with eng.Fori(0, TILES) as k:
                    n = TILES * K + k
                    eng.wait_ge(c_tile, n + 1)
                    eng.wait_ge(c_used, n + 1)
                    eng.tensor_scalar(c_mask[:, :], c_raw, 0.0, None, ALU.is_lt).then_inc(c_dve, 1)
                    eng.tensor_scalar(c_hi[:, :], c_raw, 0.0, None, ALU.min).then_inc(c_dve, 1)
                    eng.wait_ge(c_dve, 3 * n + 2)
                    eng.scalar_tensor_tensor(c_lo[:, :], c_raw, 0.0, c_hi[:, :].bitcast(fp32),
                                             ALU.min, ALU.subtract).then_inc(c_dve, 1)
                eng.wait_ge(c_used, TILES * (K + 1) + 1)
                eng.tensor_copy(minus_sb[:, :], EA[0][:, :]).then_inc(c_out, 1)
                eng.tensor_copy(ncount_sb[:, :], EA[1][0:1, :]).then_inc(c_out, 1)
                eng.tensor_copy(nvalue_sb[:, :], EB[1][:, :]).then_inc(c_out, 1)

            def last_steps(q, K, flag):
                if q == DVE_FLAG:
                    eng.wait_ge(s_above_t, K + 1)
                    links[0] = 0
                    link(eng.reduce_max(above_all[:, :], EB[0][0:1, 0:P], AX.X), K)
                    eng.tensor_scalar(has_minus[0:1, bass.ds(K, 1)], above_all[:, :], 0.0, None,
                                      ALU.is_gt).then_inc(s_flag, 1)
                if q == DVE_BRANCH:
                    flag = load_flag(eng, K)
                    with eng.If(flag > 0):
                        correct(K)
                    with eng.Else():
                        eng.sem_inc(c_dve, 3 * TILES)
                        eng.sem_inc(c_out, 3)
                if q == DVE_EXPO:
                    eng.wait_ge(s_ep_out, 2 * CH * (K + 1) + 1)
                    seen(eng)
                    with eng.If(flag > 0):
                        eng.tensor_copy(cnt[:, :, 1:2], vals[:, :, 195:196]).then_inc(s_dve, 1)
                    with eng.Else():
                        eng.memset(cnt[:, :, 1:2], 0.0).then_inc(s_dve, 1)
                    links[0] += 1
                    mark(eng.tensor_copy(cnt[:, :, 0:1], vals[:, :, 194:195]))
                    mark(eng.scalar_tensor_tensor(leaky[:, :, :], vals[:, :, 192:194], ALPHA, vals[:, :, 192:194],
                                                  ALU.mult, ALU.max))
                    join(K)
                    mark(eng.tensor_scalar(absent[:, :, :], cnt[:, :, 0:2], 0.0, 4 * NEG_INF, ALU.is_le, ALU.mult))
                    mark(eng.tensor_tensor(cnt[:, :, 2:3], cnt[:, :, 0:1], cnt[:, :, 1:2], ALU.add))
                    join(K)
                    mark(eng.tensor_tensor(leaky[:, :, :], leaky[:, :, :], absent[:, :, :], ALU.add))
                    mark(eng.tensor_scalar(cnt[:, :, 2:3], cnt[:, :, 2:3], -1.0, float(N), ALU.mult, ALU.add))
                    join(K)
                    mark(eng.scalar_tensor_tensor(top[:, :, :], leaky[:, :, 0:1], NEG_INF, leaky[:, :, 1:2],
                                                  ALU.max, ALU.max))
                    join(K)
                    eng.tensor_tensor(expo[:, :, 0:2], leaky[:, :, :], bc(top[:, :, :], 2),
                                      ALU.subtract).then_inc(s_expo, 1)
                    eng.tensor_scalar(expo[:, :, 2:3], top[:, :, :], -1.0, NEG_INF, ALU.mult, ALU.add).then_inc(s_expo, 1)
                if q == DVE_ATT:
                    eng.wait_ge(s_exp, K + 1)
                    link(eng.tensor_tensor(cnt[:, :, :], cnt[:, :, :], expo[:, :, :], ALU.mult), K)
                    link(eng.reduce_sum(norm[:, :, :], cnt[:, :, :], AX.X), K)
                    link(eng.reciprocal(norm[:, :, :], norm[:, :, :]), K)
                    link(eng.tensor_tensor(att[:, :, 0:2], expo[:, :, 0:2], bc(norm[:, :, :], 2), ALU.mult), K)
                    mark(eng.tensor_tensor(att[:, :, 2:3], att[:, :, 1:2], att[:, :, 0:1], ALU.subtract))
                    for c in range(CH):
                        g3 = gates[:, c, 0:3, H:P]
                        v3 = vals[:, c, 0:3 * H].rearrange("p (g f) -> p g f", g=3)
                        eng.scalar_tensor_tensor(g3, v3, att[:, c, 0:1], g3, ALU.mult, ALU.add).then_inc(s_gin, 1)
                    with eng.If(flag > 0):
                        eng.wait_ge(s_gin, 2 * CH * K + CH)
                        join(K)
                        seen(eng)
                        for c in range(CH):
                            g3 = gates[:, c, 0:3, H:P]
                            v3 = vals[:, c, 196:196 + 3 * H].rearrange("p (g f) -> p g f", g=3)
                            eng.scalar_tensor_tensor(g3, v3, att[:, c, 2:3], g3, ALU.mult, ALU.add).then_inc(s_gin, 1)
                    with eng.Else():
                        eng.sem_inc(s_gin, CH)
                if q == DVE_N:
                    eng.wait_ge(s_act, 3 * K + 1)
                    link(eng.scalar_tensor_tensor(gates[:, :, 3, :], gates[:, :, 1, :], 1.0, gates[:, :, 3, :],
                                                  ALU.add, ALU.mult), K)
                    eng.scalar_tensor_tensor(gates[:, :, 0, :], gates[:, :, 3, :], 0.5, gates[:, :, 0, :],
                                             ALU.mult, ALU.add).then_inc(s_nin, 1)
                    assert links[0] == PER_BLOCK - 2 * CH, links[0]
                if q == DVE_NORM:
                    links[0] = PER_BLOCK - 2 * CH
                    eng.wait_ge(s_y, K + 1)
                    if q >= UNITS:
                        seen(eng)
                    moments_of_y(mark, join, K)
                if q == DVE_X1:
                    eng.wait_ge(s_x1r, 2 * (K + 1))
                    x1b = x1_rows[:, bass.ds(CH * K, CH), :]
                    x1h = x1_split[:, bass.ds(CH * K, CH), 0:H]
                    eng.tensor_copy(x1h, x1b).then_inc(s_x1, 1)
                    eng.wait_ge(s_x1, 2 * K + 1)
                    eng.tensor_tensor(x1_split[:, bass.ds(CH * K, CH), H:2 * H], x1b, x1h.bitcast(fp32),
                                      ALU.subtract).then_inc(s_x1, 1)
                return flag

            def largest(K):
                eng.wait_ge(s_lo, UNITS * (K + 1))
                eng.reduce_max(above_max[:, :], above[:, :], AX.X).then_inc(s_above, 1)

            def one_block(I, K):
                flag = None
                for q in range(UNITS):
                    g = UNITS * I + q
                    if q == 0 and K is not None:
                        largest(K)
                    eng.wait_ge(s_tile, g + 1)
                    eng.wait_ge(s_hi, g + 1)
                    eng.tensor_scalar(mask[:, q % RING, :], raw[:, q % RAW, :], 0.0, None,
                                      ALU.is_gt).then_inc(s_mask, 1)
                    if q == 0 and K is not None:
                        eng.wait_ge(s_above, K + 1)
                        seen(eng)
                    eng.tensor_tensor_reduce(out=lo[:, q % RING, :], in0=raw[:, q % RAW, :],
                                             in1=hi[:, q % RING, :].bitcast(fp32), scale=1.0, scalar=-3.0e38,
                                             op0=ALU.subtract, op1=ALU.max,
                                             accum_out=above[:, q:q + 1]).then_inc(s_lo, 1)
                    if K is not None:
                        if not isinstance(I, int):
                            last_steps(q + UNITS, I - 2, None)
                        flag = last_steps(q, K, flag)
                    else:
                        first_steps(q)

            one_block(0, None)
            one_block(1, 0)
            with eng.Fori(2, BLOCKS) as I:
                one_block(I, I - 1)

            def sum_rows(k):
                eng.wait_ge(s_fin, k + 1)
                axp = bank[2 + k % 2][:, 0:CH * H].rearrange("p (c f) -> p c f", c=CH)
                eng.scalar_tensor_tensor(sq[:, :, :], axp, 0.01, x1_rows[:, CH * ORDER2[k]:CH * (ORDER2[k] + 1), :],
                                         ALU.mult, ALU.mult).then_inc(s_fin_rd, 1)
                eng.wait_ge(s_fin_rd, k + 1)
                eng.reduce_sum(row_sum[:, :, :], sq[:, :, :], AX.X).then_inc(s_sum, 1)

            def moments2(k):
                eng.wait_ge(s_y, BLOCKS + k + 1)
                moments_of_y(mark2, join2, None)

            flag = None
            largest(BLOCKS - 1)
            for n, (k, J, h) in enumerate(UNITS2):
                eng.wait_ge(s_hi2, n + 1)
                eng.tensor_tensor(lo[:, n % RING, :], raw[:, n % RAW, :], hi[:, n % RING, :].bitcast(fp32),
                                  ALU.subtract).then_inc(s_lo2, 1)
                last_steps(n + UNITS, BLOCKS - 2, None)
                for q in stretched(n):
                    flag = last_steps(q, BLOCKS - 1, flag)
                for k, step in ended(n, *DVE_END):
                    (sum_rows, moments2)[step](k)

        @block.tensor
        def _(eng):
            def mm(o, w, v, start=False, stop=True):
                return eng.matmul(o, w, v, start=start, stop=stop, skip_group_check=True)

            for count in (s_ep, s_ep_out, c_used):
                eng.sem_inc(count, 1)
            eng.wait_ge(s_const, 7)

            def chunk(c, K, flag):
                cs = slice(c * P, (c + 1) * P)
                A, B = EA[c % 2], EB[c % 2]
                gate3 = A[:, 0:3 * P].rearrange("p (g n) -> p g n", g=3)[:, :, 0:H]
                if c >= 2:
                    eng.wait_ge(s_ep_out, 2 * (CH * K + c - 1) + 1)
                mm(A[:, :], ones[0:H, :], bias_split[:, :], start=True)
                mm(A[:, P:4 * P], xt_split[:, cs], w_h_hi[:, :])
                mm(A[:, P:4 * P], xt_split[:, cs], w_h_lo[:, :])
                mm(gate3, plus_sb[:, cs], w_plus[:, :].rearrange("p (g f) -> p g f", g=3))
                with eng.If(flag > 0):
                    mm(gate3, minus_sb[:, cs], w_minus[:, :].rearrange("p (g f) -> p g f", g=3))
                    mm(B[:, 196:196 + 3 * H], nvalue_sb[:, cs], w_value[:, :], start=True)
                    mm(B[:, 195:196], ncount_sb[:, cs], ident[0:1, 0:1], start=True)
                    mm(B[:, 192:194], minus_sb[:, cs], a_minus[:, :], start=True)
                    mm(B[:, 192:194], plus_sb[:, cs], a_plus[:, :])
                with eng.Else():
                    mm(B[:, 192:194], plus_sb[:, cs], a_plus[:, :], start=True)
                mm(B[:, 194:195], count_sb[:, cs], quarters[:, :], start=True)
                mm(B[:, 0:3 * H], value_sb[:, cs], w_value[:, :], start=True).then_inc(s_ep, 1)

            def last_steps(q, K, flag):
                if q == PE_ABOVE:
                    eng.wait_ge(s_above, K + 1)
                    eng.wait_ge(s_ep_out, 2 * CH * K + 1)
                    eng.transpose(EB[0][0:1, 0:P], above_max[:, :], ident[:, :]).then_inc(s_above_t, 1)
                if q == PE_FLAG:
                    flag = load_flag(eng, K)
                    with eng.If(flag > 0):
                        for k in range(TILES):
                            eng.wait_ge(c_dve, 3 * (TILES * K + k + 1))
                            mm(EA[0][:, :], h_split[:, k, :], c_mask[:, :], start=(k == 0))
                            mm(EA[1][:, :], ones[:, :], c_mask[:, :], start=(k == 0))
                            mm(EB[1][:, :], h_split[:, k, :], c_hi[:, :], start=(k == 0))
                            mm(EB[1][:, :], h_split[:, k, :], c_lo[:, :]).then_inc(c_used, 1)
                    with eng.Else():
                        eng.sem_inc(c_used, TILES)
                if q == PE_CHUNKS[0]:
                    eng.wait_ge(s_evac, 4 * (K + 1))
                    eng.wait_ge(c_out, 3 * (K + 1))
                    eng.wait_ge(s_xt, K + 1)
                for c in range(CH):
                    if q == PE_CHUNKS[c]:
                        chunk(c, K, flag)
                return flag

            mask16 = mask[:, :, :].bitcast(bf16).rearrange("p s (n two) -> p s n two", two=2)

            def count_pair(q, K):
                if q == 1 and K is not None:
                    eng.wait_ge(s_evac, 4 * K + 2)
                for k in range(2 * UT):
                    last = mm(COUNT[k * P // 4:(k + 1) * P // 4, :], ones16[:, :],
                              mask16[:, (q - 1 + k // UT) % RING, (k % UT) * BI:(k % UT + 1) * BI, 1],
                              start=(q == 1))
                last.then_inc(s_free, 1)

            def tiles_of(q):
                return [(UT * unit_at(q) + t, slice(t * BI, (t + 1) * BI), q == 0 and t == 0)
                        for t in range(UT)]

            def plus(q, g):
                eng.wait_ge(s_mask, g + 1)
                for j, v, first in tiles_of(q):
                    mm(PLUS[:, :], h_split[:, j, :], mask[:, q % RING, v], start=first)

            def one_block(I, K):
                flag = None
                for q in range(UNITS):
                    g = UNITS * I + q
                    u = unit_at(q)
                    J, s = u // UPB, q % RING
                    parts = tiles_of(q)
                    if K is None and q == 0:
                        eng.wait_ge(s_h_first, 2)
                    if K is None and q == UPB:
                        eng.wait_ge(s_h_rest, 2)
                    if q == 0:
                        if K is not None:
                            eng.wait_ge(s_evac, 4 * K + 1)
                        plus(0, g)
                        plus(1, g + 1)
                    elif q > 1:
                        plus(q, g)
                    if q % 2 == 1:
                        count_pair(q, K)
                    eng.wait_ge(s_lo, g + 1)
                    if K is not None and J + 1 < BLOCKS - 1:
                        with eng.If(I > J + 1):
                            eng.wait_ge(s_x1, 2 * (J + 1))
                            for j, v, first in parts:
                                mm(AX1[:, :], x1_split[:, j, :], hi[:, s, v])
                                mm(AX1[:, :], x1_split[:, j, :], lo[:, s, v])
                    if q == 0 and K is not None:
                        eng.wait_ge(s_evac, 4 * K + 3)
                    for j, v, first in parts:
                        mm(VALUE[:, :], h_split[:, j, :], hi[:, s, v], start=first)
                        last = mm(VALUE[:, :], h_split[:, j, :], lo[:, s, v])
                    if q == 0:
                        if K is not None:
                            eng.wait_ge(s_evac, 4 * K + 4)
                        mm(AX1[:, :], zero_w[:, :], hi[:, s, 0:BI], start=True)
                    if q % 2 == 1:
                        last.then_inc(s_free, 1)
                    if K is not None:
                        flag = last_steps(q, K, flag)
                    elif q == 10:
                        eng.wait_ge(s_setup_d, 7 * 16)
                        mm(EA[0][:, 0:3 * H + 2], w_gat_t[:, :], gat[:, :], start=True).then_inc(s_w, 1)

            one_block(0, None)
            eng.wait_ge(s_wsplit, 8)
            with eng.Fori(1, BLOCKS) as I:
                one_block(I, I - 1)

            eng.wait_ge(s_evac, 4 * (BLOCKS - 1) + 2)

            def finish(k):
                I = ORDER2[k]
                eng.wait_ge(s_ax_sb, k + 1)
                if k >= 2:
                    eng.wait_ge(s_fin_rd, k - 1)
                for c in range(CH):
                    o = bank[2 + k % 2][:, c * H:(c + 1) * H]
                    if I >= 2:
                        mm(o, ax_part[:, I - 2, c * P:(c + 1) * P], pair_ident[:, :], start=True)
                    last = mm(o, ax_sb[:, c * P:(c + 1) * P], pair_ident[:, :], start=(I < 2))
                last.then_inc(s_fin, 1)

            flag = None
            for n, (k, J, h) in enumerate(UNITS2):
                sums, s = bank[k % 2], n % RING
                if n == FIRST2[k] and k >= 2:
                    eng.wait_ge(s_ax_sb, k - 1)
                if h == 0:
                    eng.wait_ge(s_x1, 2 * (J + 1))
                eng.wait_ge(s_lo2, n + 1)
                for t in range(UT):
                    j = UT * (UPB * J + h) + t
                    v = slice(t * BI, (t + 1) * BI)
                    mm(sums[:, :], x1_split[:, j, :], hi[:, s, v], start=(n == FIRST2[k] and t == 0))
                    last = mm(sums[:, :], x1_split[:, j, :], lo[:, s, v])
                last.then_inc(s_free, 1)
                if n < UNITS:
                    flag = last_steps(n, BLOCKS - 1, flag)
                for k, _ in ended(n, PE_END):
                    finish(k)


def kernel(x, adj, L0_gnn_W_gat, L0_gnn_a_gat, L0_gnn_w_ih_e, L0_gnn_w_hh_e, L0_gnn_b_ih_e,
           L0_gnn_b_hh_e, L0_gnn_w_ih_n, L0_gnn_w_hh_n, L0_gnn_b_ih_n, L0_gnn_b_hh_n, L1_gnn_t):
    import numpy as np
    import concourse.bacc as bacc
    from concourse.bass_utils import run_bass_kernel_spmd as run

    N, H = x.shape
    P, BI, UT = 128, 512, 2
    B = N // BI
    x, adj = np.asarray(x), np.asarray(adj)

    def gates(e, n, parts):
        e3, n3 = (np.asarray(a).T.reshape(-1, 3, H) for a in (e, n))
        full = np.zeros((e3.shape[0], 4, 2, H), np.float32)
        for third, part in enumerate(parts):
            full[:, part, 0] = e3[:, third]
            full[:, part, 1] = n3[:, third]
        return full.reshape(-1, 8 * H)

    def n_first(w):
        return np.concatenate([w[:, 2 * H:], w[:, :2 * H]], axis=1)

    w_ih_e, w_ih_n = (n_first(np.asarray(w).T) for w in (L0_gnn_w_ih_e, L0_gnn_w_ih_n))
    w_h = gates(L0_gnn_w_hh_e, L0_gnn_w_hh_n, (1, 2, 3))[:, 2 * H:]
    b_hh = gates(np.asarray(L0_gnn_b_hh_e)[:, None], np.asarray(L0_gnn_b_hh_n)[:, None], (1, 2, 3))
    b_ih = gates(np.asarray(L0_gnn_b_ih_e)[:, None], np.asarray(L0_gnn_b_ih_n)[:, None], (1, 2, 0))
    bias = np.zeros((H, 8 * H), np.float32)
    bias[0:2] = bias[32:34] = np.concatenate([b_hh, b_ih])
    a = np.asarray(L0_gnn_a_gat).reshape(2, H).T
    w_gat_t = np.asarray(L0_gnn_W_gat).T
    xt = np.ascontiguousarray(x.T).reshape(H, B, BI).transpose(1, 0, 2)
    arrays = {
        "adj_t": adj.reshape(B, BI, N // (UT * P), UT, P).transpose(0, 2, 4, 3, 1),
        "x_rows_d": x.reshape(N // P, P, H).transpose(1, 0, 2),
        "x_t_d": np.concatenate([xt, xt], axis=1),
        "diag_d": np.diagonal(adj).reshape(N // P, P).T,
        "gat_d": np.concatenate([w_ih_n, a], axis=1),
        "w_gat_t_d": np.concatenate([w_gat_t, w_gat_t], axis=1),
        "w_plus_d": np.concatenate([w_ih_e[:H], w_ih_e[:H]]),
        "w_minus_d": np.concatenate([w_ih_e[H:], w_ih_e[H:]]),
        "w_h_d": np.concatenate([w_h, w_h]),
        "bias_d": bias,
    }
    arrays = {name: np.ascontiguousarray(v) for name, v in arrays.items()}
    nc = bacc.Bacc("TRN2", target_bir_lowering=False, num_devices=1)
    args = [nc.dram_tensor(name, v.shape, mybir.dt.from_np(v.dtype), kind="ExternalInput").ap()
            for name, v in arrays.items()]
    out = nc.dram_tensor("out", (N, H), mybir.dt.float32, kind="ExternalOutput").ap()
    gnn_ode_kernel(nc, *args, out)
    return run(nc, [arrays], core_ids=[0]).results[0]["out"]
```
